# Optimizing a Trainium2 kernel written in Bass

```python
import numpy as np
import jax
import jax.numpy as jnp

def _softmax(x, axis=-1):
    return jax.nn.softmax(x, axis=axis)

def _gelu(x):
    return jax.nn.gelu(x, approximate=True)

def _silu(x):
    return jax.nn.silu(x)

def _sigmoid(x):
    return jax.nn.sigmoid(x)

def _layernorm(x, axis=-1, eps=1e-05):
    m = jnp.mean(x, axis=axis, keepdims=True)
    v = jnp.var(x, axis=axis, keepdims=True)
    return (x - m) / jnp.sqrt(v + eps)

def _scatter_add(tgt, idx, src, axis=0):
    return tgt.at[idx].add(src)

def _segment_sum(src, seg, n):
    return jax.ops.segment_sum(src, seg, n)
kernel_name = 'mk_rec_standalone_d1_rec_r8_f9ca40'

def setup_inputs(seed: int=0):
    np.random.seed(seed)
    _w = jnp.asarray

    def _rec_inputs():
        import jax
        import jax.numpy as jnp
        _rk = jax.random.key(seed)
        r_user_idx = jax.random.randint(jax.random.fold_in(_rk, 1), (512,), 72, 99964, jnp.int32)
        r_context_idx = jnp.stack([jax.random.randint(jax.random.fold_in(jax.random.fold_in(_rk, 2), 0), (512,), 6, 49981, jnp.int32), jax.random.randint(jax.random.fold_in(jax.random.fold_in(_rk, 2), 1), (512,), 42, 49942, jnp.int32), jax.random.randint(jax.random.fold_in(jax.random.fold_in(_rk, 2), 2), (512,), 28, 6250, jnp.int32)], axis=1)
        return (r_user_idx, r_context_idx)
    r_user_idx, r_context_idx = _rec_inputs()

    def _L0_rec_setup():
        import jax, jax.numpy as jnp
        import numpy as np
        NUM_USERS = 12500
        NUM_SERVICES = 6250
        EMB_DIM = 32
        CONTEXT = 3
        NUM_EDGES = 200000
        BATCH = 256

        def gcn_conv(x, W, b, src, dst, n):
            h = x @ W
            loops = jnp.arange(n, dtype=src.dtype)
            s = jnp.concatenate([src, loops])
            d = jnp.concatenate([dst, loops])
            ones = jnp.ones(s.shape[0], dtype=x.dtype)
            deg = jax.ops.segment_sum(ones, d, num_segments=n)
            dis = jnp.where(deg > 0, jax.lax.rsqrt(jnp.maximum(deg, 1e-12)), 0.0)
            norm = dis[s] * dis[d]
            msgs = h[s] * norm[:, None]
            out = jax.ops.segment_sum(msgs, d, num_segments=n)
            return out + b
        key = jax.random.key(seed)
        ks = jax.random.split(key, 12)
        user_idx = jax.random.randint(ks[0], (BATCH,), 0, NUM_USERS)
        context_idx = jax.random.randint(ks[1], (BATCH, CONTEXT), 0, NUM_SERVICES)
        edge_index = jax.random.randint(ks[2], (2, NUM_EDGES), 0, NUM_SERVICES)
        s = 1.0 / np.sqrt(EMB_DIM)
        user_emb = jax.random.normal(ks[3], (NUM_USERS, EMB_DIM), jnp.float32)
        service_emb = jax.random.normal(ks[4], (NUM_SERVICES, EMB_DIM), jnp.float32)
        W1 = jax.random.normal(ks[5], (EMB_DIM, EMB_DIM), jnp.float32) * s
        b1 = jnp.zeros((EMB_DIM,), jnp.float32)
        W2 = jax.random.normal(ks[6], (EMB_DIM, EMB_DIM), jnp.float32) * s
        b2 = jnp.zeros((EMB_DIM,), jnp.float32)
        fin = EMB_DIM * (CONTEXT + 1)
        fc_W = jax.random.normal(ks[7], (fin, NUM_SERVICES), jnp.float32) / np.sqrt(fin)
        fc_b = jnp.zeros((NUM_SERVICES,), jnp.float32)
        return {'user_idx': user_idx, 'context_idx': context_idx, 'edge_index': edge_index, 'user_emb': user_emb, 'service_emb': service_emb, 'W1': W1, 'b1': b1, 'W2': W2, 'b2': b2, 'fc_W': fc_W, 'fc_b': fc_b}
    _L0_rec_all = _L0_rec_setup()
    _L0_rec_in = {k: v for k, v in _L0_rec_all.items() if k in ('edge_index', 'user_emb', 'service_emb', 'W1', 'b1', 'W2', 'b2', 'fc_W', 'fc_b')}
    del _L0_rec_all
    return {'r_user_idx': r_user_idx, 'r_context_idx': r_context_idx, 'L0_rec_edge_index': _L0_rec_in['edge_index'], 'L0_rec_user_emb': _L0_rec_in['user_emb'], 'L0_rec_service_emb': _L0_rec_in['service_emb'], 'L0_rec_W1': _L0_rec_in['W1'], 'L0_rec_b1': _L0_rec_in['b1'], 'L0_rec_W2': _L0_rec_in['W2'], 'L0_rec_b2': _L0_rec_in['b2'], 'L0_rec_fc_W': _L0_rec_in['fc_W'], 'L0_rec_fc_b': _L0_rec_in['fc_b']}

def reference(r_user_idx, r_context_idx, L0_rec_edge_index, L0_rec_user_emb, L0_rec_service_emb, L0_rec_W1, L0_rec_b1, L0_rec_W2, L0_rec_b2, L0_rec_fc_W, L0_rec_fc_b):
    import jax
    import jax.numpy as jnp

    def _L0_rec_ref(user_idx, context_idx, edge_index, user_emb, service_emb, W1, b1, W2, b2, fc_W, fc_b):
        import jax, jax.numpy as jnp
        import numpy as np
        NUM_USERS = 12500
        NUM_SERVICES = 6250
        EMB_DIM = 32
        CONTEXT = 3
        NUM_EDGES = 200000
        BATCH = 256

        def gcn_conv(x, W, b, src, dst, n):
            h = x @ W
            loops = jnp.arange(n, dtype=src.dtype)
            s = jnp.concatenate([src, loops])
            d = jnp.concatenate([dst, loops])
            ones = jnp.ones(s.shape[0], dtype=x.dtype)
            deg = jax.ops.segment_sum(ones, d, num_segments=n)
            dis = jnp.where(deg > 0, jax.lax.rsqrt(jnp.maximum(deg, 1e-12)), 0.0)
            norm = dis[s] * dis[d]
            msgs = h[s] * norm[:, None]
            out = jax.ops.segment_sum(msgs, d, num_segments=n)
            return out + b
        src, dst = (edge_index[0], edge_index[1])
        user_vec = user_emb[user_idx]
        g = jax.nn.relu(gcn_conv(service_emb, W1, b1, src, dst, NUM_SERVICES))
        g = gcn_conv(g, W2, b2, src, dst, NUM_SERVICES)
        ctx = g[context_idx].reshape(context_idx.shape[0], -1)
        x = jnp.concatenate([user_vec, ctx], axis=1)
        return x @ fc_W + fc_b
    y = _L0_rec_ref(r_user_idx, r_context_idx, L0_rec_edge_index, L0_rec_user_emb, L0_rec_service_emb, L0_rec_W1, L0_rec_b1, L0_rec_W2, L0_rec_b2, L0_rec_fc_W, L0_rec_fc_b)
    return y

_drawn_inputs = setup_inputs


def setup_inputs(seed=0):
    import zlib

    import numpy as np

    out = dict(_drawn_inputs(seed))
    spreads = {'L0_rec_b1': (0.0, 0.1), 'L0_rec_b2': (0.0, 0.1), 'L0_rec_fc_b': (0.0, 0.1)}
    factors = {}
    for name, (base, spread) in spreads.items():
        noise = np.random.default_rng([zlib.crc32(name.encode()), seed]).standard_normal(out[name].shape)
        drawn = base * np.exp(spread * noise) if base else spread * noise
        out[name] = jnp.asarray(drawn.astype(out[name].dtype))
    for name, factor in factors.items():
        out[name] = (out[name] * factor).astype(out[name].dtype)
    return out
```

```python
import concourse.bass as bass
from concourse import mybir
from contextlib import ExitStack

F32 = mybir.dt.float32
F16 = mybir.dt.float16
BF16 = mybir.dt.bfloat16
FP8 = mybir.dt.float8e4
I32 = mybir.dt.int32
I16 = mybir.dt.int16
U8 = mybir.dt.uint8
ALU = mybir.AluOpType
ACT = mybir.ActivationFunctionType

P = 128
D = 32
D3 = 3 * D
N = 6250
NH = -(-N // P)
FULL = N // P
TAIL = N - FULL * P
NP = NH * P
E = 200000
EC = E // P
ET = E - EC * P
JH = -(-(EC + 1) // P)
T = JH * P
CH = 250
NC = N // CH
NB = NC * NH
R = 3
TW = 70
GB = 7
NG = NH // GB
OP = TW // NG
UN = (NH + 1) // 2
BANKS = 5
ADJ = -(-NH * CH // 32) * 32
NR = 3
DEPTH = 4195
DSHIFT = 19
G = 16
DG = -(-(EC + 1) // G)
MULT = 8
U = 8
GT = -(-(EC + 1) // U) * U
TURNS_G = GT // U
BATCH = 512
BB = BATCH // P
CTX = 3
USERS = 12500
BANK = 512
K_SRC, K_DST, K_BLK, K_CH = 0, 7, 15, 21
GUARD = 1 << 29
PAD_CH, PAD_BLK = 31, 63
LEVELS = (P * 2048).bit_length() - 1
PLO = 7


def float_of_bits(bits):
    import numpy as np
    return float(np.array([bits], np.int32).view(np.float32)[0])


def sort_plan():
    plan, domain = [], "T"
    for level in range(1, LEVELS + 1):
        for bit in range(level - 1, -1, -1):
            d = "T" if bit < PLO else "J"
            if d != domain:
                plan.append(("turn", level, domain))
                domain = d
            plan.append(("stage", level, bit, bit == level - 1 and level > 1, d))
    plan.append(("turn", LEVELS + 1, "T"))
    return plan


def gcn_kernel(nc, user_idx, context_idx, edge_index, user_emb, service_emb,
               W1, b1, W2, b2, fc_W, fc_b, out):
    table = nc.dram_tensor("context_table", (NP, D), F32).ap()
    spill = nc.dram_tensor("adjacency_spill", (NC, P, ADJ), U8).ap()
    messages = nc.dram_tensor("message_table", (NP, D), F32).ap()
    PLAN = sort_plan()
    CHUNKS = [(c, min(BANK, T - c)) for c in range(0, T, BANK)]
    NQ = len(CHUNKS)
    NCH = [(c, min(BANK, N - c)) for c in range(0, N, BANK)]
    ZC = [(c, min(16, NH - c)) for c in range(0, NH, 16)]
    TC = [(c, min(BANK, (NC + 1) * NH - c)) for c in range(0, (NC + 1) * NH, BANK)]

    ctx = ExitStack()
    with ctx:
        def sem(name):
            return ctx.enter_context(nc.semaphore(name))

        def sb(name, shape, dt, where=ctx):
            return where.enter_context(nc.sbuf_tensor(name, shape, dt))

        ident = sb("ident", [P, P], F32)
        identb = sb("identb", [P, P], BF16)
        iota_lo = sb("iota_lo", [P, P], F32)
        chan = sb("chan", [P, 1], F32)
        iota_src_flat = sb("iota_src", [P, NH * P * R], I16)
        iota_src = iota_src_flat[:].rearrange("p (a l r) -> p a l r", l=P, r=R)
        iota_dst = sb("iota_dst", [P, CH, OP], I16)
        dst16 = sb("dst16", [P, T], I16)
        src16 = sb("src16", [P, T], I16)
        chunk16 = sb("chunk16", [P, T], I16)
        window = sb("window", [P, 2, TW], I16)
        oh_src = sb("oh_src", [P, GB, P, R], F16)
        tab = sb("tab", [1, NC, NG, 8], I32)
        parts = sb("parts", [P, NH, 3, D], BF16)
        YT = sb("YT", [D3, NP], F32)
        deg = sb("deg", [P, NH], F32)
        dis = sb("dis", [P, NH], F32)
        tmp49 = sb("tmp49", [P, NH], F32)
        W1s = sb("W1s", [D3, D], F32)
        W2s = sb("W2s", [D3, D], F32)
        bias = sb("bias", [P, 2, D], F32)
        adj_flat = sb("adj", [P, NR * ADJ], U8)
        adj = adj_flat[:].rearrange("p (k n) -> p k n", k=NR)
        adj8 = [adj[:, k, :].bitcast(FP8) for k in range(NR)]
        codes = adj[:, 0, 0:(NC + 1) * NH * 4].bitcast(F32)
        before = adj[:, 1, 0:2 * (NC + 1) * NH * 2].bitcast(F16).rearrange("p (b n) -> p b n", b=2)
        X0 = adj[:, 2, 0:NH * D * 4].bitcast(F32).rearrange("p (h f) -> p h f", f=D)
        tau = adj[0:1, 2, NH * D * 4:NH * D * 4 + (NC + 1) * NH * 4].bitcast(F32)
        uidx = sb("uidx", [P, BB], I32)
        cidx = sb("cidx", [P, BB, CTX], I32)
        idx_f = sb("idx_f", [P, BB * (CTX + 1)], F32)
        neg_f = sb("neg_f", [P, BB * (CTX + 1)], F32)
        ucl = sb("ucl", [P, BB], I32)
        ccl = sb("ccl", [P, BB * CTX], I32)
        feat = sb("feat", [P, BB, P], F32)
        ones16 = sb("ones16", [P, 1], F16)

        last_code = sb("last_code", [P, JH], F32)
        last_i = sb("last_i", [P, JH], I32)
        zero_row = sb("zero_row", [1, P], F16)
        cnum = sb("cnum", [P, NC + 1], F32)

        bad = sb("bad", [1, 1], I32)
        worst = sb("worst", [1, 4], F32)
        dup = sb("dup", [P, 1], F32)
        ones32 = sb("ones32", [P, 1], F32)
        spare = iota_src_flat[:, 0:12 * GT].bitcast(F32).rearrange("p (k n) -> p k n", n=GT)
        g_lo, g_hi, g_src = spare[:, 0, :], spare[:, 1, :], spare[:, 2, :].bitcast(I32)
        g_hi_wide, g_x, g_y = (spare[:, k, :].rearrange("p (h f) -> p h f", f=D) for k in (3, 4, 5))
        room = adj_flat[:].bitcast(F32)
        g_spread = [room[:, k * GT:(k + 1) * GT].rearrange("p (h f) -> p h f", f=D) for k in range(2)]
        g_int = [room[:, k * GT:(k + 1) * GT].bitcast(I32) for k in range(2)]
        g_oh = [room[:, 2 * GT + k * P:2 * GT + (k + 1) * P] for k in range(2)]
        g_rows = [room[:, 2 * GT + 2 * P + k * D:2 * GT + 2 * P + (k + 1) * D] for k in range(U)]
        g_stage = room[:, 2 * GT + 2 * P + U * D:2 * GT + 2 * P + U * D + U].bitcast(I32)
        g_zero = room[0:1, 2 * GT + 2 * P + U * D + U:2 * GT + 2 * P + U * D + U + BANK]
        with ExitStack() as early:
            dst_i = sb("dst_i", [P, T], I32, early)
            src_i = sb("src_i", [P, T], I32, early)
            key_i = sb("key_i", [P, T], I32, early)
            keys = [sb(f"keys{k}", [P, T], F32, early) for k in range(2)]
            lo16 = sb("lo16", [P, DG * G], I16, early)
            hi16 = sb("hi16", [P, DG * G], I16, early)
            iota_l = sb("iota_l", [P, P, G], I16, early)
            iota_h = sb("iota_h", [P, NH, G], I16, early)
            oh_lo = sb("oh_lo", [P, 2, P, G], F16, early)
            oh_hi = sb("oh_hi", [P, 2, NH, G], F16, early)
            sign = sb("sign", [P, PLO], F32, early)
            chan_i = sb("chan_i", [P, PLO], I32, early)
            bit_i = sb("bit_i", [P, PLO], I32, early)
        with ExitStack() as early:
            hot = sb("hot", [P, 2, CH, TW], F16, early)
        with ExitStack() as late:
            fcW = sb("fcW", [P, N], F32, late)
            fcb = sb("fcb", [P, N], F32, late)
            res = sb("res", [P, 4, BANK], F32, late)
            featT = sb("featT", [P, BATCH], F32, late)
            X = sb("X", [P, NH, D], F32, late)
        ps = [ctx.enter_context(nc.psum_tensor(f"ps{k}", [P, BANK], F32)) for k in range(BANKS)]
        psY = ctx.enter_context(nc.psum_tensor("psY", [P, NR, BANK], F32))
        psD = ps[4]
        psC = [psY[0:1, 0, 0:TC[0][1]], psY[0:1, 1, 0:TC[1][1]], psY[0:1, 2, 0:TC[2][1]]]

        TH = [(h, min(4, NH - h)) for h in range(0, NH, 4)]
        psT = [ps[k][0:D3, :].bitcast(BF16) for k in range(2)]

        edges_in, nodes_in, weights_in, heads_in, fc_in = map(sem, ("edges_in", "nodes_in", "weights_in", "heads_in", "fc_in"))
        edges_set, consts, iotas, sorted_to, turned, moved = map(sem, ("edges_set", "consts", "iotas", "sorted_to", "turned", "moved"))
        oh_ready, oh_used, deg_sum, root_in, root_out = map(sem, ("oh_ready", "oh_used", "deg_sum", "root_in", "root_out"))
        dup_ready, dup_summed = map(sem, ("dup_ready", "dup_summed"))
        chain, before_ready, counted, tab_ready, unpacked = map(sem, ("chain", "before_ready", "counted", "tab_ready", "unpacked"))
        parts_ready, yt_turned, yt_set = map(sem, ("parts_ready", "yt_turned", "yt_set"))
        hot_ready, src_ready, win_ready, block_done, evicted = map(sem, ("hot_ready", "src_ready", "win_ready", "block_done", "evicted"))
        y_done, y_added, spilled = map(sem, ("y_done", "y_added", "spilled"))
        z_done, table_ready, table_out, clamped, rows_in = map(sem, ("z_done", "table_ready", "table_out", "clamped", "rows_in"))
        feat_T, feat_copied, fc_mm, res_ready = map(sem, ("feat_T", "feat_copied", "fc_mm", "res_ready"))
        loaded = [sem(f"loaded{k}") for k in range(NR)]
        stored = [sem(f"stored{k}") for k in range(4)]

        def walk(on_stage, on_turn):
            stages = turns = 0
            for n, step in enumerate(PLAN):
                if step[0] == "stage":
                    on_stage(step, n % 2, stages, turns)
                    stages += 1
                else:
                    on_turn(step, n % 2, stages, turns)
                    turns += 1
            return stages, turns

        g_edges, g_set, g_parted, g_x_ready, g_table, g_staged, g_stage_free = map(sem, ("g_edges", "g_set", "g_parted", "g_x_ready", "g_table", "g_staged", "g_stage_free"))
        g_slot_free, g_spread_ready, g_mm, g_summed, g_y_ready, g_turned, g_added, g_turn, g_wide = map(sem, ("g_slot_free", "g_spread_ready", "g_mm", "g_summed", "g_y_ready", "g_turned", "g_added", "g_turn", "g_wide"))
        g_rows_in = [sem(f"g_rows_in{k}") for k in range(U)]
        held = {e: sem(f"held_{e}") for e in ("sp", "act", "dve", "pe")}

        def hold(eng, name):
            eng.sem_inc(held[name], 1)

        skip = lambda *a: None
        STAGES, TURNS = walk(skip, skip)
        sorted_keys, sorted_rows = keys[len(PLAN) % 2], keys[(len(PLAN) - 1) % 2]

        def deg_groups(turn_step, turns, at=[0]):
            done = sum(2 if s[2] == "T" else 7 for s in [s for s in PLAN if s[0] == "turn"][:turns])
            n = 2 if turn_step[2] == "T" else 7
            return min(done, DG), min(done + n, DG)

        block = ctx.enter_context(nc.Block())

        @block.sync
        def _(sp):
            def store_messages(layer):
                sp.wait_ge(g_x_ready, layer + 1)
                sp.dma_start(messages.rearrange("(h l) f -> l h f", l=P), g_x).then_inc(g_table, 16)
                sp.wait_ge(g_table, 16 * (layer + 1))

            sp.wait_ge(edges_set, 1)
            for row, tile in ((1, dst_i), (0, src_i)):
                sp.dma_start(tile[:, 0:EC], edge_index[row, 0:EC * P].rearrange("(p t) -> p t", p=P)).then_inc(edges_in, 16)
                sp.dma_start(tile[0:ET, EC:EC + 1], edge_index[row, EC * P:E].rearrange("(p t) -> p t", t=1)).then_inc(edges_in, 16)
            sp.dma_start(X0[:, 0:FULL, :], service_emb[0:FULL * P, :].rearrange("(h l) f -> l h f", l=P)).then_inc(nodes_in, 16)
            sp.dma_start(X0[0:TAIL, FULL, :], service_emb[FULL * P:N, :]).then_inc(nodes_in, 16)
            for k in range(3):
                sp.dma_start(W1s[k * D:(k + 1) * D, :], W1).then_inc(weights_in, 16)
                sp.dma_start(W2s[k * D:(k + 1) * D, :], W2).then_inc(weights_in, 16)
            sp.dma_start(bias[:, 0, :], b1[None, :].to_broadcast((P, D))).then_inc(weights_in, 16)
            sp.dma_start(bias[:, 1, :], b2[None, :].to_broadcast((P, D))).then_inc(weights_in, 16)
            sp.dma_start(uidx[:], user_idx.rearrange("(p b) -> p b", p=P)).then_inc(heads_in, 16)
            sp.dma_start(cidx[:], context_idx.rearrange("(p b) c -> p b c", p=P)).then_inc(heads_in, 16)
            sp.wait_ge(tab_ready, 1)
            is_bad = nc.sync.value_load(bad[:], min_val=0, max_val=1)
            with sp.If(is_bad == 0):
                with sp.Fori(0, NC - NR) as c:
                    sp.wait_ge(evicted, BANKS + (c + 1) * UN)
                    sp.dma_start(spill[bass.ds(c, 1), :, 0:NH * CH].rearrange("a p n -> (a p) n"),
                                 adj[:, bass.ds(c % NR, 1), 0:NH * CH].rearrange("p a n -> p (a n)")).then_inc(spilled, 16)
                    sp.wait_ge(spilled, c * 16 + 16)
                    hold(sp, "sp")
            with sp.Else():
                sp.wait_ge(g_set, 1)
                for row, tile in ((1, g_int[0]), (0, g_src)):
                    sp.dma_start(tile[:, 0:EC], edge_index[row, 0:EC * P].rearrange("(p t) -> p t", p=P)).then_inc(g_edges, 16)
                    sp.dma_start(tile[0:ET, EC:EC + 1], edge_index[row, EC * P:E].rearrange("(p t) -> p t", t=1)).then_inc(g_edges, 16)
                store_messages(0)
            sp.wait_ge(y_done, NC)
            sp.dma_start(fcW[:], fc_W).then_inc(fc_in, 16)
            sp.dma_start(fcb[:], fc_b[None, :].to_broadcast((P, N))).then_inc(fc_in, 16)

            def bring(i, j):
                sp.wait_ge(y_done, NC + (i - NR + 1))
                hold(sp, "sp")
                c = NC - 1 - i
                slot = (NC - 1 - j) % NR
                src = spill[bass.ds(c, 1), :, 0:NH * CH].rearrange("a p n -> (a p) n")
                sp.dma_start(adj[:, slot, 0:NH * CH], src).then_inc(loaded[j % NR], 16)

            with sp.If(is_bad == 0):
                with sp.Fori(1, NC // NR) as t:
                    for j in range(NR):
                        bring(t * NR + j, j)
                for i in range(NC // NR * NR, NC):
                    bring(i, i)
            with sp.Else():
                store_messages(1)
            sp.wait_ge(table_ready, 1)
            sp.dma_start(table.rearrange("(h l) f -> l h f", l=P), X[:]).then_inc(table_out, 16)
            sp.wait_ge(table_out, 16)
            n = 0
            out_v = out.rearrange("(p b) n -> p b n", b=BB)
            for b in range(BB):
                for c, w in NCH:
                    sp.wait_ge(res_ready, n + 1)
                    sp.dma_start(out_v[:, b, c:c + w], res[:, n % 4, 0:w]).then_inc(stored[n % 4], 16)
                    n += 1
            for k in range(4):
                sp.wait_ge(stored[k], 16 * len(range(k, n, 4)))

        @block.gpsimd
        def _(pool):
            def iota(tile, pattern, base, mult):
                return nc.gpsimd.iota(tile, pattern=pattern, base=base, channel_multiplier=mult,
                                      allow_small_or_imprecise_dtypes=True)
            iota(iota_lo[:], [[1, P]], 0, 0)
            iota(chan_i[:], [[0, PLO]], 0, 1)
            iota(cnum[:], [[1, NC + 1]], 0, 0)
            iota(chan[:], [[0, 1]], 0, 1).then_inc(consts, 1)
            iota(iota_l[:], [[1, P], [0, G]], 0, 0)
            iota(iota_h[:], [[1, NH], [0, G]], 0, 0).then_inc(iotas, 1)
            iota(codes, [[64, NC + 1], [1, NH]], 0, 0).then_inc(iotas, 1)
            iota(iota_dst[:], [[1, CH], [0, OP]], 0, 0)
            iota(iota_src, [[P, NH], [1, P], [0, R]], 1, 0).then_inc(iotas, 1)
            pool.wait_ge(clamped, 1)
            for b in range(BB):
                nc.gpsimd.indirect_dma_start(feat[:, b, 0:D], None, user_emb,
                    bass.IndirectOffsetOnAxis(ap=ucl[:, b:b + 1], axis=0)).then_inc(rows_in, 16)
            pool.wait_ge(tab_ready, 1)
            is_bad = nc.gpsimd.value_load(bad[:], min_val=0, max_val=1)
            with pool.If(is_bad == 1):
                iota(g_hi_wide, [[1, NH], [0, D]], 0, 0).then_inc(g_wide, 1)
                for layer in range(2):
                    pool.wait_ge(g_table, 16 * (layer + 1))
                    with pool.Fori(0, TURNS_G) as i:
                        pool.wait_ge(g_staged, i + (1 + layer * TURNS_G))
                        for j in range(U):
                            pool.wait_ge(g_slot_free, i * U + (j + 1 + layer * GT))
                            pool.sem_inc(g_turn, 1)
                            nc.gpsimd.indirect_dma_start(g_rows[j], None, messages,
                                bass.IndirectOffsetOnAxis(ap=g_stage[:, j:j + 1], axis=0)).then_inc(g_rows_in[j], 16)
            pool.wait_ge(table_out, 16)
            for b in range(BB):
                for c in range(CTX):
                    nc.gpsimd.indirect_dma_start(feat[:, b, D * (c + 1):D * (c + 2)], None, table,
                        bass.IndirectOffsetOnAxis(ap=ccl[:, b * CTX + c:b * CTX + c + 1], axis=0)).then_inc(rows_in, 16)

        @block.scalar
        def _(act):
            def on_turn(step, cur, stages, turns):
                dst = keys[1 - cur]
                _, level, left = step
                half = 1 << max(level + 1 - PLO - 1, 0)
                for q, (c, w) in enumerate(CHUNKS):
                    act.wait_ge(turned, NQ * turns + q + 1)
                    if left == "T" or level == LEVELS:
                        ins = nc.scalar.copy(dst[:, c:c + w], ps[q][:, 0:w])
                    elif half < P:
                        ins = nc.scalar.activation(dst[:, c:c + w], ps[q][:, 0:w], ACT.Copy,
                                                   scale=sign[:, level - PLO:level - PLO + 1])
                    else:
                        for b in range(w // P):
                            s = -1.0 if ((c // P + b) // (half // P)) % 2 else 1.0
                            ins = nc.scalar.mul(dst[:, c + b * P:c + (b + 1) * P], ps[q][:, b * P:(b + 1) * P], s)
                    ins.then_inc(moved, 1)
            walk(skip, on_turn)
            act.wait_ge(root_in, 1)
            nc.scalar.activation(dis[:], tmp49[:], ACT.Sqrt).then_inc(root_out, 1)

            def set_yt(layer):
                for k, (h, w) in enumerate(TH):
                    act.wait_ge(yt_turned, layer * len(TH) + k + 1)
                    nc.scalar.copy(YT[:, h * P:(h + w) * P], psT[k % 2][:, 0:w * P]).then_inc(yt_set, 1)
            set_yt(0)

            def chunk(c, slot, first):
                for u in range(UN):
                    w = min(2, NH - 2 * u)
                    if u == 0 and not first:
                        act.wait_ge(spilled, 16 * (c - NR + 1))
                        act.wait_ge(y_done, c - NR + 1)
                    act.wait_ge(block_done, GB + c * NH + 2 * u + w)
                    hold(act, "act")
                    nc.scalar.activation(adj8[slot][:, u * 2 * CH:(u * 2 + w) * CH],
                                         ps[u % BANKS][:, 0:w * CH], ACT.Copy, saturate=False).then_inc(evicted, 1)
            act.wait_ge(tab_ready, 1)
            is_bad = nc.scalar.value_load(bad[:], min_val=0, max_val=1)
            with act.If(is_bad == 0):
                act.sem_inc(evicted, BANKS)
                for c in range(NR):
                    chunk(c, c, True)
                with act.Fori(1, NC // NR) as t:
                    for k in range(NR):
                        chunk(t * NR + k, k, False)
                for c in range(NC // NR * NR, NC):
                    chunk(c, c % NR, False)
            with act.Else():
                for layer in range(2):
                    act.wait_ge(g_table, 16 * (layer + 1))
                    with act.Fori(0, TURNS_G) as i:
                        act.wait_ge(g_stage_free, i + (1 + layer * TURNS_G))
                        nc.scalar.copy(g_stage, g_src[:, bass.ds(i * U, U)]).then_inc(g_staged, 1)
                    if layer == 0:
                        set_yt(1)
            with act.If(is_bad == 0):
                set_yt(1)

        @block.vector
        def _(dve):
            n_chain = [0]

            def link(ins):
                n_chain[0] += 1
                ins.then_inc(chain, 1)
                dve.wait_ge(chain, n_chain[0])

            V = nc.vector
            V.memset(X0[:, FULL, :], 0.0)
            V.memset(ones16[:], 1.0)
            V.memset(ones32[:], 1.0)
            V.memset(zero_row[:], 0.0)
            V.memset(src_i[:, EC:T], 0)
            V.memset(dst_i[:, EC:T], -P).then_inc(edges_set, 1)
            dve.wait_ge(consts, 1)
            for q in range(PLO):
                V.tensor_scalar(bit_i[:, q:q + 1], chan_i[:, q:q + 1], q, 1, ALU.arith_shift_right, ALU.bitwise_and)
            V.tensor_scalar(identb[:], iota_lo[:], chan[:], None, ALU.is_equal)
            link(V.tensor_scalar(ident[:], iota_lo[:], chan[:], None, ALU.is_equal))
            link(V.tensor_scalar(sign[:], bit_i[:], -2.0, 1.0, ALU.mult, ALU.add))
            dve.wait_ge(heads_in, 32)
            for lo, cnt, src, dst, size in ((0, BB, uidx[:], ucl[:], USERS), (BB, BB * CTX, cidx[:].rearrange("p b c -> p (b c)"), ccl[:], N)):
                f, g = idx_f[:, lo:lo + cnt], neg_f[:, lo:lo + cnt]
                link(V.tensor_copy(f, src))
                link(V.tensor_scalar(g, f, 0.0, float(size), ALU.is_lt, ALU.mult))
                link(V.tensor_tensor(f, f, g, ALU.add))
                link(V.tensor_scalar(f, f, 0.0, float(size - 1), ALU.max, ALU.min))
                link(V.tensor_copy(dst, f))
            dve.sem_inc(clamped, 1)
            dve.wait_ge(edges_in, 64)
            k0, k1 = keys[0][:].bitcast(I32), keys[1][:].bitcast(I32)
            link(V.tensor_scalar(key_i[:], dst_i[:], 1, None, ALU.arith_shift_right))
            link(V.tensor_scalar(key_i[:], key_i[:], float(DEPTH), None, ALU.mult))
            link(V.tensor_scalar(k0, key_i[:], DSHIFT, None, ALU.arith_shift_right))
            link(V.scalar_tensor_tensor(out=key_i[:], in0=k0, scalar=-float(CH), in1=dst_i[:], op0=ALU.mult, op1=ALU.add))
            V.tensor_scalar(k0, k0, K_CH, None, ALU.logical_shift_left)
            V.tensor_scalar(k1, src_i[:], P - 1, GUARD, ALU.bitwise_and, ALU.bitwise_or)
            link(V.tensor_scalar(key_i[:], key_i[:], K_DST, None, ALU.logical_shift_left))
            V.tensor_tensor(k0, k0, k1, ALU.bitwise_or)
            link(V.tensor_scalar(src_i[:], src_i[:], K_BLK - PLO, 63 << K_BLK, ALU.logical_shift_left, ALU.bitwise_and))
            link(V.tensor_tensor(key_i[:], key_i[:], src_i[:], ALU.bitwise_or))
            link(V.tensor_tensor(key_i[:], key_i[:], k0, ALU.bitwise_or))
            pad = float_of_bits(GUARD | PAD_CH << K_CH | PAD_BLK << K_BLK)
            V.memset(key_i[ET:P, EC:EC + 1].bitcast(F32), pad)
            link(V.memset(key_i[:, EC + 1:T].bitcast(F32), pad))
            V.tensor_scalar(keys[0][:], key_i[:].bitcast(F32), sign[:, 0:1], None, ALU.mult).then_inc(sorted_to, 1)
            dve.wait_ge(sorted_to, 1)
            link(V.tensor_scalar(key_i[:, 0:DG * G], dst_i[:, 0:DG * G], P - 1, None, ALU.bitwise_and))
            V.tensor_copy(lo16[:], key_i[:, 0:DG * G])
            link(V.tensor_scalar(src_i[:, 0:DG * G], dst_i[:, 0:DG * G], PLO, None, ALU.arith_shift_right))
            link(V.tensor_copy(hi16[:], src_i[:, 0:DG * G]))
            dve.wait_ge(iotas, 1)

            def exchange(o_low, o_high, low, high, turned_sign):
                if turned_sign:
                    V.scalar_tensor_tensor(out=o_low, in0=high, scalar=-1.0, in1=low, op0=ALU.mult, op1=ALU.min)
                    return V.scalar_tensor_tensor(out=o_high, in0=high, scalar=-1.0, in1=low, op0=ALU.mult, op1=ALU.max)
                V.tensor_tensor(o_low, low, high, ALU.min)
                return V.tensor_tensor(o_high, low, high, ALU.max)

            def on_stage(step, cur, stages, turns):
                _, level, bit, mirror, domain = step
                s, t = keys[cur], keys[1 - cur]
                dve.wait_ge(sorted_to, stages + 1)
                dve.wait_ge(moved, NQ * turns) if turns else None
                h = 1 << (bit if domain == "T" else bit - PLO)
                whole = T // (2 * h)
                rest = T - whole * 2 * h
                neg = mirror and domain == "J"
                way = slice(None, None, -1) if mirror else slice(None)
                if whole:
                    sv = s[:, 0:whole * 2 * h].rearrange("p (q two h) -> p q two h", two=2, h=h)
                    tv = t[:, 0:whole * 2 * h].rearrange("p (q two h) -> p q two h", two=2, h=h)
                    ins = exchange(tv[:, :, 0, :], tv[:, :, 1, way], sv[:, :, 0, :], sv[:, :, 1, way], neg)
                if rest:
                    o = whole * 2 * h
                    w = max(rest - h, 0)
                    a = o + (h - w if mirror else 0)
                    if w:
                        ins = exchange(t[:, a:a + w], t[:, o + h:o + rest][:, way], s[:, a:a + w], s[:, o + h:o + rest][:, way], neg)
                    c0, c1 = (o, o + min(rest, h) - w) if mirror or not w else (o + w, o + h)
                    if c1 > c0:
                        ins = V.tensor_copy(t[:, c0:c1], s[:, c0:c1])
                ins.then_inc(sorted_to, 1)

            def on_turn(step, cur, stages, turns):
                for g in range(*deg_groups(step, turns)):
                    if g >= 2:
                        dve.wait_ge(oh_used, g - 1)
                    for oh, it, v, n in ((oh_lo, iota_l, lo16, P), (oh_hi, iota_h, hi16, NH)):
                        ins = V.tensor_tensor(oh[:, g % 2, :, :], it[:], v[:, g * G:(g + 1) * G].rearrange("p (o r) -> p o r", o=1).to_broadcast((P, n, G)), ALU.is_equal)
                    ins.then_inc(oh_ready, 1)
            walk(on_stage, on_turn)
            dve.wait_ge(iotas, 3)
            dve.wait_ge(sorted_to, STAGES + 1)
            rows = sorted_rows[:].rearrange("p (j t) -> p j t", t=P)
            same = dst_i[:, 0:JH * (P - MULT)].bitcast(F32).rearrange("p (j t) -> p j t", t=P - MULT)
            link(V.tensor_tensor(same, rows[:, :, MULT:P], rows[:, :, 0:P - MULT], ALU.is_equal))
            V.scalar_tensor_tensor(out=same, in0=rows[:, :, MULT:P], scalar=pad, in1=same, op0=ALU.is_lt, op1=ALU.mult,
                                   accum_out=dup[:]).then_inc(dup_ready, 1)
            dve.wait_ge(dup_ready, 1)
            link(V.tensor_scalar(last_i[:], rows[:, :, P - 1].bitcast(I32), K_BLK, 2047, ALU.arith_shift_right, ALU.bitwise_and))
            link(V.tensor_copy(last_code[:], last_i[:]))
            for j in range(JH):
                if j >= 2:
                    dve.wait_ge(counted, j - 1)
                V.tensor_scalar(before[:, j % 2, :], codes, last_code[:, j:j + 1], None, ALU.is_gt).then_inc(before_ready, 1)
            dve.wait_ge(moved, NQ * TURNS)
            sk = sorted_keys[:].bitcast(I32)
            V.tensor_scalar(dst_i[:], sk, K_DST, 255, ALU.arith_shift_right, ALU.bitwise_and)
            V.tensor_scalar(src_i[:], sk, K_BLK - PLO, 63 << PLO, ALU.arith_shift_right, ALU.bitwise_and)
            link(V.tensor_scalar(key_i[:], sk, P - 1, None, ALU.bitwise_and))
            V.tensor_copy(dst16[:], dst_i[:])
            link(V.tensor_tensor(src_i[:], src_i[:], key_i[:], ALU.bitwise_or))
            V.tensor_scalar(src16[:], src_i[:], 1.0, None, ALU.add)
            link(V.tensor_scalar(key_i[:], sk, K_CH, 31, ALU.arith_shift_right, ALU.bitwise_and))
            link(V.tensor_copy(chunk16[:], key_i[:]))
            dve.wait_ge(deg_sum, 2)
            link(V.tensor_scalar(deg[:], psD[:, 0:NH], 1.0, None, ALU.add))
            V.reciprocal(tmp49[:], deg[:]).then_inc(root_in, 1)
            dve.wait_ge(root_out, 1)
            link(V.tensor_tensor(tmp49[:], dis[:], dis[:], ALU.mult))
            link(V.tensor_tensor(tmp49[:], tmp49[:], deg[:], ALU.mult))
            link(V.tensor_scalar(tmp49[:], tmp49[:], -0.5, 1.5, ALU.mult, ALU.add))
            link(V.tensor_tensor(dis[:], dis[:], tmp49[:], ALU.mult))
            dis_w = dis[:].rearrange("p (h o) -> p h o", o=1).to_broadcast((P, NH, D))

            def split(x, last):
                for k in range(3):
                    if k == 2:
                        V.tensor_copy(parts[:, :, k, :], x).then_inc(parts_ready, 1)
                    else:
                        link(V.tensor_copy(parts[:, :, k, :], x))
                        link(V.tensor_tensor(x, x, parts[:, :, k, :], ALU.subtract))
            dve.wait_ge(nodes_in, 32)
            link(V.tensor_tensor(X0, X0, dis_w, ALU.mult))
            split(X0, 0)
            dve.wait_ge(counted, JH)
            for k, (c, w) in enumerate(TC):
                ins = V.tensor_copy(tau[:, c:c + w], psC[k])
            link(ins)
            tv = tau[:, 0:NB].rearrange("p (c b) -> p c b", b=NH)
            nxt = tau[:, NH:NB + NH].rearrange("p (c b) -> p c b", b=NH)[:, :, 0:1]
            V.tensor_tensor(tab[:, :, :, 0:GB], tv.rearrange("p c (g j) -> p c g j", j=GB),
                            tv[:, :, 0:1].rearrange("p c (g j) -> p c g j", j=1).to_broadcast((1, NC, NG, GB)), ALU.subtract)
            link(V.tensor_copy(tab[:, :, :, GB], nxt.to_broadcast((1, NC, NG))))
            diff = key_i[0:1, 0:NB].bitcast(F32)
            chunk_diff = key_i[0:1, NB:NB + NC].bitcast(F32)
            V.tensor_copy(worst[:, 3:4], psD[0:1, 64:65])
            link(V.tensor_tensor(diff, tau[:, 1:NB + 1], tau[:, 0:NB], ALU.subtract))
            V.tensor_reduce(worst[:, 0:1], diff, axis=mybir.AxisListType.X, op=ALU.max)
            link(V.tensor_tensor(chunk_diff, nxt, tv[:, :, 0:1], ALU.subtract))
            link(V.tensor_reduce(worst[:, 1:2], chunk_diff, axis=mybir.AxisListType.X, op=ALU.max))
            link(V.tensor_scalar(worst[:, 0:1], worst[:, 0:1], -float(R - 1), None, ALU.add))
            link(V.tensor_scalar(worst[:, 1:2], worst[:, 1:2], -float(TW - R), None, ALU.add))
            link(V.tensor_tensor(worst[:, 0:1], worst[:, 0:1], worst[:, 1:2], ALU.max))
            link(V.tensor_tensor(worst[:, 0:1], worst[:, 0:1], worst[:, 3:4], ALU.max))
            link(V.tensor_scalar(bad[:], worst[:, 0:1], 0.0, None, ALU.is_gt))
            dve.sem_inc(tab_ready, 1)
            dve.sem_inc(y_added, NR)
            dve.wait_ge(yt_set, len(TH))

            regs = [dve.alloc_register(f"visit{k}") for k in range(GB + 1)]

            def general(layer):
                V.tensor_tensor(g_x, parts[:, :, 1, :], parts[:, :, 2, :], ALU.add).then_inc(g_added, 1)
                dve.wait_ge(g_added, 1 + layer * (NH + 1))
                V.tensor_tensor(g_x, g_x, parts[:, :, 0, :], ALU.add).then_inc(g_x_ready, 1)
                dve.wait_ge(g_wide, 1)
                with dve.Fori(0, TURNS_G) as i:
                    for j in range(U):
                        dve.wait_ge(g_rows_in[j], i * 16 + 16 * (1 + layer * TURNS_G))
                        dve.wait_ge(g_mm, i * U + (j + 1 + layer * GT))
                        V.tensor_scalar(g_oh[j % 2], iota_lo[:], g_lo[:, bass.ds(i * U + j, 1)], None, ALU.is_equal)
                        rows = g_rows[j].rearrange("p (o f) -> p o f", o=1).to_broadcast((P, NH, D))
                        V.scalar_tensor_tensor(out=g_spread[j % 2], in0=g_hi_wide, scalar=g_hi[:, bass.ds(i * U + j, 1)], in1=rows,
                                               op0=ALU.is_equal, op1=ALU.mult).then_inc(g_spread_ready, 1)
                        dve.wait_ge(g_spread_ready, i * U + (j + 1 + layer * GT))
                        dve.sem_inc(g_slot_free, 1)
                    dve.sem_inc(g_stage_free, 1)
                dve.wait_ge(g_summed, layer + 1)
                for k, (c, w) in enumerate(ZC):
                    ins = V.tensor_copy(g_y[:, c:c + w, :], ps[k][:, 0:w * D].rearrange("p (h f) -> p h f", f=D))
                ins.then_inc(g_y_ready, 1)
                for h in range(NH):
                    dve.wait_ge(g_turned, layer * NH + h + 1)
                    y = YT[0:D, h * P:(h + 1) * P]
                    V.tensor_tensor(y, y, psY[0:D, h % 2, 0:P], ALU.add).then_inc(g_added, 1)
                dve.wait_ge(g_added, (layer + 1) * (NH + 1))
                dve.sem_inc(y_added, NC)

            def next_window(c, base):
                return V.scalar_tensor_tensor(out=window[:, c % 2, :] if isinstance(c, int) else window[:, bass.ds(c % 2, 1), :].rearrange("p a t -> p (a t)"),
                                              in0=chunk16[:, bass.ds(base, TW)], scalar=cnum[:, bass.ds(c, 1)], in1=src16[:, bass.ds(base, TW)],
                                              op0=ALU.is_equal, op1=ALU.mult).then_inc(win_ready, 1)

            def next_hot(c, base, g):
                o = hot[:, bass.ds(c % 2, 1), :, g * OP:(g + 1) * OP].rearrange("p a d t -> p (a d) t")
                return V.tensor_tensor(o, iota_dst[:], dst16[:, bass.ds(base + g * OP, OP)].rearrange("p (o t) -> p o t", o=1).to_broadcast((P, CH, OP)),
                                       ALU.is_equal).then_inc(hot_ready, 1)

            def add_y(c, count):
                dve.wait_ge(y_done, count)
                y = YT[:, bass.ds(c * CH, CH)]
                V.tensor_tensor(y, y, psY[0:D3, bass.ds(c % NR, 1), 0:CH].rearrange("p a n -> p (a n)"), ALU.add).then_inc(y_added, 1)

            def chunk(c, first, last):
                for g in range(NG):
                    V.load(regs, tab[0:1, bass.ds(c, 1), g, :].rearrange("p a j -> p (a j)"))
                    at = [dve.snap(r, min_val=0, max_val=TW - R) for r in regs[0:GB]]
                    base = dve.snap(regs[GB], min_val=0, max_val=T - TW)
                    if not last:
                        if g == 0:
                            dve.wait_ge(block_done, GB + c * NH)
                            next_window(c + 1, base)
                        next_hot(c + 1, base, g)
                    if g == 2 and not first:
                        add_y(c - 1, c)
                    if g == 0:
                        dve.wait_ge(win_ready, c + 1)
                    for j in range(GB):
                        b = g * GB + j
                        dve.wait_ge(block_done, c * NH + b + 1)
                        V.tensor_tensor(oh_src[:, j, :, :], iota_src[:, b, :, :],
                                        window[:, bass.ds(c % 2, 1), bass.ds(at[j], R)].to_broadcast((P, P, R)),
                                        ALU.is_equal).then_inc(src_ready, 1)
            is_bad = nc.vector.value_load(bad[:], min_val=0, max_val=1)
            with dve.If(is_bad == 0):
                next_window(0, 0)
                for g in range(NG):
                    next_hot(0, 0, g)
                chunk(0, True, False)
                with dve.Fori(1, NC - 1) as c:
                    chunk(c, False, False)
                chunk(NC - 1, False, True)
                add_y(NC - 1, NC)
            with dve.Else():
                V.memset(g_zero, 0.0)
                V.memset(g_src[:, EC:GT], 0)
                V.memset(g_int[0][:, EC:GT], -P).then_inc(g_set, 1)
                dve.wait_ge(g_edges, 64)
                dve.wait_ge(g_set, 1)
                for k, (shift, mask, o) in enumerate(((0, P - 1, g_lo), (PLO, -1, g_hi))):
                    if k:
                        dve.wait_ge(g_parted, 2 * k)
                    V.tensor_scalar(g_int[1], g_int[0], shift, mask, ALU.arith_shift_right, ALU.bitwise_and).then_inc(g_parted, 1)
                    dve.wait_ge(g_parted, 2 * k + 1)
                    V.tensor_copy(o, g_int[1]).then_inc(g_parted, 1)
                dve.wait_ge(g_parted, 4)
                general(0)

            def finish(layer):
                dve.wait_ge(z_done, layer + 1)
                for k, (c, w) in enumerate(ZC):
                    ins = V.tensor_tensor(X[:, c:c + w, :], ps[k][:, 0:w * D].rearrange("p (h f) -> p h f", f=D), dis_w[:, c:c + w, :], ALU.mult)
                link(ins)
                return V.tensor_tensor(X[:], X[:], bias[:, layer:layer + 1, :].to_broadcast((P, NH, D)), ALU.add)
            dve.wait_ge(weights_in, 16 * 8)
            link(finish(0))
            link(V.scalar_tensor_tensor(out=X[:], in0=X[:], scalar=0.0, in1=dis_w, op0=ALU.max, op1=ALU.mult))
            split(X[:], 1)
            dve.wait_ge(yt_set, 2 * len(TH))
            is_bad = nc.vector.value_load(bad[:], min_val=0, max_val=1)
            with dve.If(is_bad == 0):
                with dve.Fori(0, NC) as i:
                    dve.wait_ge(y_done, NC + (i + 1))
                    hold(dve, "dve")
                    y = YT[:, bass.ds((NC - 1 - i) * CH, CH)]
                    V.tensor_tensor(y, y, psY[0:D3, bass.ds((NC + i) % NR, 1), 0:CH].rearrange("p a n -> p (a n)"), ALU.add).then_inc(y_added, 1)
            with dve.Else():
                general(1)
            finish(1).then_inc(table_ready, 1)

            for b in range(BB):
                dve.wait_ge(feat_T, b + 1)
                V.tensor_copy(featT[:, b * P:(b + 1) * P], psY[:, b % 2, 0:P]).then_inc(feat_copied, 1)
            dve.wait_ge(fc_in, 32)
            n = 0
            for b in range(BB):
                for c, w in NCH:
                    dve.wait_ge(fc_mm, n + 1)
                    if n >= 4:
                        dve.wait_ge(stored[n % 4], 16 * (n // 4))
                    V.tensor_tensor(res[:, n % 4, 0:w], ps[n % 4][:, 0:w], fcb[:, c:c + w], ALU.add).then_inc(res_ready, 1)
                    n += 1

        @block.tensor
        def _(pe):
            MM = nc.tensor.matmul
            pe.wait_ge(sorted_to, 1)

            def on_turn(step, cur, stages, turns):
                src = keys[cur]
                pe.wait_ge(sorted_to, stages + 1)
                for q, (c, w) in enumerate(CHUNKS):
                    if turns:
                        pe.wait_ge(moved, NQ * (turns - 1) + q + 1)
                    for b in range(w // P):
                        ins = nc.tensor.transpose(ps[q][:, b * P:(b + 1) * P], src[:, c + b * P:c + (b + 1) * P], ident[:])
                    ins.then_inc(turned, 1)
                g0, g1 = deg_groups(step, turns)
                if g0 == 0 and g1 > 0:
                    MM(psD[:, 0:NH], zero_row[0:1, 0:P], zero_row[0:1, 0:NH], start=True, stop=False)
                if g1 > g0:
                    with pe.Fori(g0, g1) as g:
                        pe.wait_ge(oh_ready, g + 1)
                        for t in range(G):
                            ins = MM(psD[:, 0:NH], oh_lo[:, bass.ds(g % 2, 1), :, t].rearrange("p a n -> p (a n)"),
                                     oh_hi[:, bass.ds(g % 2, 1), :, t].rearrange("p a n -> p (a n)"), start=False, stop=False)
                        ins.then_inc(oh_used, 1)
            walk(skip, on_turn)
            MM(psD[:, 0:NH], zero_row[0:1, 0:P], zero_row[0:1, 0:NH], start=False, stop=True).then_inc(deg_sum, 1)
            pe.wait_ge(dup_ready, 1)
            MM(psD[0:1, 64:65], ones32[:], dup[:], start=True, stop=True).then_inc(deg_sum, 1)
            pe.wait_ge(moved, NQ * TURNS)
            for j in range(JH):
                pe.wait_ge(before_ready, j + 1)
                for k, (c, w) in enumerate(TC):
                    ins = MM(psC[k], ones16[:], before[:, j % 2, c:c + w], start=(j == 0), stop=(j == JH - 1))
                ins.then_inc(counted, 1)

            def turn_parts(layer):
                pe.wait_ge(parts_ready, layer + 1)
                for k, (h, w) in enumerate(TH):
                    if k >= 2:
                        pe.wait_ge(yt_set, layer * len(TH) + k - 1)
                    for b in range(w):
                        ins = nc.tensor.transpose(psT[k % 2][:, b * P:(b + 1) * P], parts[:, h + b, :, :].rearrange("p k f -> p (k f)"), identb[:])
                    ins.then_inc(yt_turned, 1)
                pe.wait_ge(yt_set, (layer + 1) * len(TH))
            turn_parts(0)
            pe.wait_ge(tab_ready, 1)
            pe.sem_inc(block_done, GB)
            regs = [pe.alloc_register(f"visit{k}") for k in range(GB)]

            def general(layer):
                pe.wait_ge(g_table, 16 * (layer + 1))
                if layer == 0:
                    pe.sem_inc(g_mm, 2)
                    pe.sem_inc(g_slot_free, U)
                    pe.sem_inc(g_stage_free, 1)
                for k, (c, w) in enumerate(ZC):
                    MM(ps[k][:, 0:w * D], g_zero[:, 0:P], g_zero[:, 0:w * D], start=True, stop=False)
                with pe.Fori(0, TURNS_G) as i:
                    for j in range(U):
                        pe.wait_ge(g_spread_ready, i * U + (j + 1 + layer * GT))
                        for k, (c, w) in enumerate(ZC):
                            ins = MM(ps[k][:, 0:w * D], g_oh[j % 2], g_spread[j % 2][:, c:c + w, :].rearrange("p h f -> p (h f)"), start=False, stop=False)
                        ins.then_inc(g_mm, 1)
                for k, (c, w) in enumerate(ZC):
                    ins = MM(ps[k][:, 0:w * D], g_zero[:, 0:P], g_zero[:, 0:w * D], start=False, stop=True)
                ins.then_inc(g_summed, 1)
                pe.wait_ge(g_y_ready, layer + 1)
                for h in range(NH):
                    if h >= 2:
                        pe.wait_ge(g_added, layer * (NH + 1) + h)
                    nc.tensor.transpose(psY[0:D, h % 2, 0:P], g_y[:, h, :], ident[:]).then_inc(g_turned, 1)
                pe.wait_ge(y_added, NR + NC * (layer + 1))
                pe.sem_inc(y_done, NC)

            def aggregate(c, slot, order, u):
                for s in range(2 * u, min(2 * u + 2, NH)):
                    ins = MM(psY[0:D3, order % NR, 0:CH], parts[:, s, :, :].rearrange("p k f -> p (k f)"),
                             adj8[slot][:, s * CH:(s + 1) * CH], start=(s == 0), stop=(s == NH - 1))
                return ins

            def chunk(c, slot):
                def unit(u):
                    if u == 0:
                        pe.wait_ge(y_added, c + 1)
                    pe.wait_ge(evicted, BANKS + c * UN + (u + 1))
                    hold(pe, "pe")
                    ins = aggregate(c, slot, slot, u)
                    if u == UN - 1:
                        ins.then_inc(y_done, 1)
                for s in range(NH):
                    u = s // 2
                    if s % GB == 0:
                        nc.tensor.load(regs, tab[0:1, bass.ds(c, 1), s // GB, 0:GB].rearrange("p a j -> p (a j)"))
                        at = [pe.snap(r, min_val=0, max_val=TW - R) for r in regs]
                    if s == 0:
                        pe.wait_ge(hot_ready, NG * (c + 1))
                    if s % 2 == 0:
                        pe.wait_ge(evicted, c * UN + (u + 1))
                    pe.wait_ge(src_ready, c * NH + (s + 1))
                    for r in range(R):
                        ins = MM(ps[u % BANKS][:, (s % 2) * CH:(s % 2 + 1) * CH], oh_src[:, s % GB, :, r],
                                 hot[:, bass.ds(c % 2, 1), :, bass.ds(at[s % GB] + r, 1)].rearrange("p a d t -> p (a d t)"),
                                 start=(r == 0), stop=(r == R - 1))
                    ins.then_inc(block_done, 1)
                    if s % 2 == 1 and u >= 2:
                        unit(u - 2)
                for u in range(UN - 3, UN):
                    unit(u)
            is_bad = nc.tensor.value_load(bad[:], min_val=0, max_val=1)
            with pe.If(is_bad == 0):
                with pe.Fori(0, NC // NR) as t:
                    for k in range(NR):
                        chunk(t * NR + k, k)
                for c in range(NC // NR * NR, NC):
                    chunk(c, c % NR)
            with pe.Else():
                general(0)

            def linear(layer, Ws):
                pe.wait_ge(y_added, NR + NC * (layer + 1))
                for h in range(NH):
                    ins = MM(ps[h // 16][:, (h % 16) * D:(h % 16 + 1) * D], YT[:, h * P:(h + 1) * P], Ws[:], start=True, stop=True)
                ins.then_inc(z_done, 1)
            pe.wait_ge(weights_in, 16 * 8)
            linear(0, W1s)
            turn_parts(1)

            def again(i, j, first):
                pe.wait_ge(y_added, NC + i + 1)
                if not first:
                    pe.wait_ge(loaded[j % NR], 16 * (i // NR) if isinstance(i, int) else 16 * turn_no[0])
                hold(pe, "pe")
                for u in range(UN):
                    ins = aggregate(None, (NC - 1 - j) % NR, NC + j, u)
                ins.then_inc(y_done, 1)
            is_bad = nc.tensor.value_load(bad[:], min_val=0, max_val=1)
            with pe.If(is_bad == 0):
                turn_no = [None]
                for j in range(NR):
                    again(j, j, True)
                with pe.Fori(1, NC // NR) as t:
                    turn_no[0] = t
                    for j in range(NR):
                        again(t * NR + j, j, False)
                for i in range(NC // NR * NR, NC):
                    again(i, i, False)
            with pe.Else():
                general(1)
            linear(1, W2s)

            pe.wait_ge(rows_in, 16 * BB * (CTX + 1))
            for b in range(BB):
                if b >= 2:
                    pe.wait_ge(feat_copied, b - 1)
                nc.tensor.transpose(psY[:, b % 2, 0:P], feat[:, b, :], ident[:]).then_inc(feat_T, 1)
            pe.wait_ge(feat_copied, BB)
            pe.wait_ge(fc_in, 32)
            n = 0
            for b in range(BB):
                for c, w in NCH:
                    if n >= 4:
                        pe.wait_ge(res_ready, n - 3)
                    MM(ps[n % 4][:, 0:w], featT[:, b * P:(b + 1) * P], fcW[:, c:c + w], start=True, stop=True).then_inc(fc_mm, 1)
                    n += 1


_INS = ['r_user_idx', 'r_context_idx', 'L0_rec_edge_index', 'L0_rec_user_emb', 'L0_rec_service_emb',
        'L0_rec_W1', 'L0_rec_b1', 'L0_rec_W2', 'L0_rec_b2', 'L0_rec_fc_W', 'L0_rec_fc_b']


def kernel(**inputs):
    import numpy as _np
    import concourse.bacc as _bacc
    from concourse import mybir as _mybir
    from concourse.bass_utils import run_bass_kernel_spmd as _run

    nc = _bacc.Bacc("TRN2", target_bir_lowering=False, num_devices=1)
    arrays, args = {}, []
    for name in _INS:
        a = _np.ascontiguousarray(inputs[name])
        arrays[f"in_{name}_dram"] = a
        args.append(nc.dram_tensor(f"in_{name}_dram", a.shape, _mybir.dt.from_np(a.dtype), kind="ExternalInput").ap())
    args.append(nc.dram_tensor("out_dram", (BATCH, N), _mybir.dt.float32, kind="ExternalOutput").ap())
    gcn_kernel(nc, *args)
    r = _run(nc, [arrays], core_ids=[0])
    return r.results[0]["out_dram"]
```

```python
import concourse.bass as bass
from concourse import mybir
from contextlib import ExitStack

F32 = mybir.dt.float32
F16 = mybir.dt.float16
BF16 = mybir.dt.bfloat16
FP8 = mybir.dt.float8e4
I32 = mybir.dt.int32
I16 = mybir.dt.int16
U8 = mybir.dt.uint8
ALU = mybir.AluOpType
ACT = mybir.ActivationFunctionType

P = 128
D = 32
D3 = 3 * D
N = 6250
NH = -(-N // P)
FULL = N // P
TAIL = N - FULL * P
NP = NH * P
E = 200000
EC = E // P
ET = E - EC * P
JH = -(-(EC + 1) // P)
T = JH * P
CH = 250
NC = N // CH
NB = NC * NH
R = 3
TW = 72
GB = 7
NG = NH // GB
LG = 3
NPC = NG - 1
OP = TW // NPC
RING = 12
UN = (NH + 1) // 2
BANKS = 5
ADJ = -(-NH * CH // 32) * 32
NR = 3
DEPTH = 4195
DSHIFT = 19
G = 16
GV = 8
DG = -(-(EC + 1) // G)
HR = 3
MULT = 8
U = 8
GT = -(-(EC + 1) // U) * U
TURNS_G = GT // U
BATCH = 512
BB = BATCH // P
CTX = 3
USERS = 12500
BANK = 512
TURN_AT = 9
K_SRC, K_DST, K_BLK, K_CH = 0, 7, 15, 21
GUARD = 1 << 29
PAD_CH, PAD_BLK = 31, 63
LEVELS = (P * 2048).bit_length() - 1
PLO = 7


def float_of_bits(bits):
    import numpy as np
    return float(np.array([bits], np.int32).view(np.float32)[0])


def sort_plan():
    plan, domain = [], "T"
    for level in range(1, LEVELS + 1):
        for bit in range(level - 1, -1, -1):
            d = "T" if bit < PLO else "J"
            if d != domain:
                plan.append(("turn", level, domain))
                domain = d
            plan.append(("stage", level, bit, bit == level - 1 and level > 1, d))
    plan.append(("turn", LEVELS + 1, "T"))
    return plan


def gcn_kernel(nc, user_idx, context_idx, edge_index, user_emb, service_emb,
               W1, b1, W2, b2, fc_W, fc_b, out):
    table = nc.dram_tensor("context_table", (NP, D), F32).ap()
    spill = nc.dram_tensor("adjacency_spill", (NC, P, ADJ), U8).ap()
    messages = nc.dram_tensor("message_table", (NP, D), F32).ap()
    PLAN = sort_plan()
    CHUNKS = [(c, min(BANK, T - c)) for c in range(0, T, BANK)]
    NQ = len(CHUNKS)
    NCH = [(c, min(BANK, N - c)) for c in range(0, N, BANK)]
    ZC = [(c, min(16, NH - c)) for c in range(0, NH, 16)]
    TC = [(c, min(BANK, (NC + 1) * NH - c)) for c in range(0, (NC + 1) * NH, BANK)]

    ctx = ExitStack()
    with ctx:
        def sem(name):
            return ctx.enter_context(nc.semaphore(name))

        def sb(name, shape, dt, where=ctx):
            return where.enter_context(nc.sbuf_tensor(name, shape, dt))

        ident = sb("ident", [P, P], F32)
        identb = sb("identb", [P, P], BF16)
        iota_lo = sb("iota_lo", [P, P], F32)
        chan = sb("chan", [P, 1], F32)
        iota_src_flat = sb("iota_src", [P, NH * P * R], I16)
        iota_src = iota_src_flat[:].rearrange("p (a l r) -> p a l r", l=P, r=R)
        iota_dst = sb("iota_dst", [P, CH, OP], I16)
        dst16 = sb("dst16", [P, T], I16)
        src16 = sb("src16", [P, T], I16)
        chunk16 = sb("chunk16", [P, T], I16)
        window = sb("window", [P, 2 * TW], I16)
        oh_src = sb("oh_src", [P, RING + 1, P, R], F16)
        parts = sb("parts", [P, NH, 3, D], BF16)
        YT = sb("YT", [P, NP], F32)
        tab = YT[D3:D3 + 1, 0:NC * NG * 8].bitcast(I32).rearrange("p (c g j) -> p c g j", g=NG, j=8)
        deg = sb("deg", [P, NH], F32)
        dis = sb("dis", [P, NH], F32)
        tmp49 = sb("tmp49", [P, NH], F32)
        W1s = sb("W1s", [D3, D], F32)
        W2s = sb("W2s", [D3, D], F32)
        bias = sb("bias", [P, 2, D], F32)
        adj_flat = sb("adj", [P, NR * ADJ], U8)
        adj = adj_flat[:].rearrange("p (k n) -> p k n", k=NR)
        adj8 = [adj[:, k, :].bitcast(FP8) for k in range(NR)]
        codes = adj[:, 0, 0:(NC + 1) * NH * 2].bitcast(I16)
        before = adj[:, 1, 0:2 * (NC + 1) * NH * 2].bitcast(F16).rearrange("p (b n) -> p b n", b=2)
        parity = adj[0:1, 0, 6144:6144 + (NC + 1) * NH * 4].bitcast(F32)
        X0 = adj[:, 2, 0:NH * D * 4].bitcast(F32).rearrange("p (h f) -> p h f", f=D)
        tau = adj[0:1, 2, NH * D * 4:NH * D * 4 + (NC + 1) * NH * 4].bitcast(F32)
        uidx = sb("uidx", [P, BB], I32)
        cidx = sb("cidx", [P, BB, CTX], I32)
        idx_f = sb("idx_f", [P, BB * (CTX + 1)], F32)
        neg_f = sb("neg_f", [P, BB * (CTX + 1)], F32)
        ucl = sb("ucl", [P, BB], I32)
        ccl = sb("ccl", [P, BB * CTX], I32)
        feat = sb("feat", [P, BB, P], F32)
        ones16 = sb("ones16", [P, 1], F16)

        last_code = sb("last_code", [P, JH], F32)
        last_i = sb("last_i", [P, JH], I32)
        cnum = sb("cnum", [P, NC + 1], F32)

        bad = sb("bad", [1, 1], I32)
        worst = sb("worst", [1, 4], F32)
        dup = sb("dup", [P, 1], F32)
        ones32 = sb("ones32", [P, 1], F32)
        spare = iota_src_flat[:, 0:12 * GT].bitcast(F32).rearrange("p (k n) -> p k n", n=GT)
        g_lo, g_hi, g_src = spare[:, 0, :], spare[:, 1, :], spare[:, 2, :].bitcast(I32)
        g_hi_wide, g_x, g_y = (spare[:, k, :].rearrange("p (h f) -> p h f", f=D) for k in (3, 4, 5))
        room = adj_flat[:].bitcast(F32)
        g_spread = [room[:, k * GT:(k + 1) * GT].rearrange("p (h f) -> p h f", f=D) for k in range(2)]
        g_int = [room[:, k * GT:(k + 1) * GT].bitcast(I32) for k in range(2)]
        g_oh = [room[:, 2 * GT + k * P:2 * GT + (k + 1) * P] for k in range(2)]
        g_rows = [room[:, 2 * GT + 2 * P + k * D:2 * GT + 2 * P + (k + 1) * D] for k in range(U)]
        g_stage = room[:, 2 * GT + 2 * P + U * D:2 * GT + 2 * P + U * D + U].bitcast(I32)
        g_zero = room[0:1, 2 * GT + 2 * P + U * D + U:2 * GT + 2 * P + U * D + U + BANK]
        with ExitStack() as early:
            dst_i = sb("dst_i", [P, T], I32, early)
            src_i = sb("src_i", [P, T], I32, early)
            key_i = sb("key_i", [P, T], I32, early)
            keys = [sb(f"keys{k}", [P, T], F32, early) for k in range(2)]
            neg_lo = sb("neg_lo", [P, DG * G], F32, early)
            hi16 = sb("hi16", [P, DG * G], I16, early)
            iota_half = sb("iota_half", [P, P], F32, early)
            iota_l = sb("iota_l", [P, P, GV], I16, early)
            lo16 = sb("lo16", [P, DG * G], I16, early)
            cum = sb("cum", [NH, P], F32, early)
            count = sb("count", [NH, P], F32, early)
            iota_h = sb("iota_h", [P, NH, G], I16, early)
            step_lo = sb("step_lo", [P, 2, G - GV, P], F16, early)
            oh_lo = sb("oh_lo", [P, HR, P, GV], F16, early)
            oh_hi = sb("oh_hi", [P, HR, NH, G], F16, early)
            zero_row = sb("zero_row", [1, 2 * P], F16, early)
            sign = sb("sign", [P, PLO], F32, early)
            chan_i = sb("chan_i", [P, PLO], I32, early)
            bit_i = sb("bit_i", [P, PLO], I32, early)
        with ExitStack() as early:
            hot = sb("hot", [P, CH * 2 * TW], F16, early)
            hot_v = hot[:].rearrange("p (d t) -> p d t", t=2 * TW)
        with ExitStack() as late:
            fcW = sb("fcW", [P, N], F32, late)
            fcb = sb("fcb", [P, N], F32, late)
            res = sb("res", [P, 4, BANK], F32, late)
            featT = sb("featT", [P, BATCH], F32, late)
            X = sb("X", [P, NH, D], F32, late)
        ps = [ctx.enter_context(nc.psum_tensor(f"ps{k}", [P, BANK], F32)) for k in range(BANKS)]
        psY = ctx.enter_context(nc.psum_tensor("psY", [P, NR, BANK], F32))
        psD = ps[4]
        psC = [psY[0:1, 0, 0:TC[0][1]], psY[0:1, 1, 0:TC[1][1]], psY[0:1, 2, 0:TC[2][1]]]

        TH = [(h, min(4, NH - h)) for h in range(0, NH, 4)]
        psT = [[b[0:D3, :].bitcast(BF16) for b in two] for two in ((ps[0], ps[1]), (ps[4], psY[:, 0, :]))]

        edges_in, nodes_in, weights_in, heads_in, fc_in = map(sem, ("edges_in", "nodes_in", "weights_in", "heads_in", "fc_in"))
        edges_set, consts, iotas, sorted_to, turned, moved = map(sem, ("edges_set", "consts", "iotas", "sorted_to", "turned", "moved"))
        hi_ready, lo_ready, oh_used, halves, cum_out, deg_sum, root_in, root_out = map(sem, ("hi_ready", "lo_ready", "oh_used", "halves", "cum_out", "deg_sum", "root_in", "root_out"))
        dup_ready, dup_summed = map(sem, ("dup_ready", "dup_summed"))
        chain, before_ready, counted, tab_ready, unpacked = map(sem, ("chain", "before_ready", "counted", "tab_ready", "unpacked"))
        dis_ready, rest_ready, part_out = map(sem, ("dis_ready", "rest_ready", "part_out"))
        parts_ready, yt_turned, yt_set = map(sem, ("parts_ready", "yt_turned", "yt_set"))
        hot_ready, src_ready, win_ready, block_done, evicted = map(sem, ("hot_ready", "src_ready", "win_ready", "block_done", "evicted"))
        y_done, y_added, spilled = map(sem, ("y_done", "y_added", "spilled"))
        z_done, table_ready, table_out, clamped, users_in = map(sem, ("z_done", "table_ready", "table_out", "clamped", "users_in"))
        rows_in = [sem(f"rows_in{b}") for b in range(BB)]
        feat_T, feat_copied, fc_mm, res_ready = map(sem, ("feat_T", "feat_copied", "fc_mm", "res_ready"))
        loaded = [sem(f"loaded{k}") for k in range(NR)]
        stored = [sem(f"stored{k}") for k in range(4)]

        def walk(on_stage, on_turn):
            stages = turns = 0
            for n, step in enumerate(PLAN):
                if step[0] == "stage":
                    on_stage(step, n % 2, stages, turns)
                    stages += 1
                else:
                    on_turn(step, n % 2, stages, turns)
                    turns += 1
            return stages, turns

        g_edges, g_set, g_parted, g_x_ready, g_table, g_staged, g_stage_free = map(sem, ("g_edges", "g_set", "g_parted", "g_x_ready", "g_table", "g_staged", "g_stage_free"))
        g_slot_free, g_spread_ready, g_mm, g_summed, g_y_ready, g_turned, g_added, g_turn, g_wide = map(sem, ("g_slot_free", "g_spread_ready", "g_mm", "g_summed", "g_y_ready", "g_turned", "g_added", "g_turn", "g_wide"))
        g_rows_in = [sem(f"g_rows_in{k}") for k in range(U)]
        held = {e: sem(f"held_{e}") for e in ("sp", "act", "dve", "pe")}

        def hold(eng, name):
            eng.sem_inc(held[name], 1)

        dis_w = dis[:].rearrange("p (h o) -> p h o", o=1).to_broadcast((P, NH, D))

        def place(b):
            return RING if b == NH - 1 else b % RING

        skip = lambda *a: None
        STAGES, TURNS = walk(skip, skip)
        sorted_keys, sorted_rows = keys[len(PLAN) % 2], keys[(len(PLAN) - 1) % 2]

        def steps_by(stages):
            return min(DG, stages * DG // (STAGES - 6))

        block = ctx.enter_context(nc.Block())

        @block.sync
        def _(sp):
            def store_messages(layer):
                sp.wait_ge(g_x_ready, layer + 1)
                sp.dma_start(messages.rearrange("(h l) f -> l h f", l=P), g_x).then_inc(g_table, 16)
                sp.wait_ge(g_table, 16 * (layer + 1))

            sp.wait_ge(edges_set, 1)
            for row, tile in ((1, dst_i), (0, src_i)):
                sp.dma_start(tile[:, 0:EC], edge_index[row, 0:EC * P].rearrange("(p t) -> p t", p=P)).then_inc(edges_in, 16)
                sp.dma_start(tile[0:ET, EC:EC + 1], edge_index[row, EC * P:E].rearrange("(p t) -> p t", t=1)).then_inc(edges_in, 16)
            sp.dma_start(X0[:, 0:FULL, :], service_emb[0:FULL * P, :].rearrange("(h l) f -> l h f", l=P)).then_inc(nodes_in, 16)
            sp.dma_start(X0[0:TAIL, FULL, :], service_emb[FULL * P:N, :]).then_inc(nodes_in, 16)
            for k in range(3):
                sp.dma_start(W1s[k * D:(k + 1) * D, :], W1).then_inc(weights_in, 16)
                sp.dma_start(W2s[k * D:(k + 1) * D, :], W2).then_inc(weights_in, 16)
            sp.dma_start(bias[:, 0, :], b1[None, :].to_broadcast((P, D))).then_inc(weights_in, 16)
            sp.dma_start(bias[:, 1, :], b2[None, :].to_broadcast((P, D))).then_inc(weights_in, 16)
            sp.dma_start(uidx[:], user_idx.rearrange("(p b) -> p b", p=P)).then_inc(heads_in, 16)
            sp.dma_start(cidx[:], context_idx.rearrange("(p b) c -> p b c", p=P)).then_inc(heads_in, 16)
            sp.wait_ge(tab_ready, 1)
            is_bad = nc.sync.value_load(bad[:], min_val=0, max_val=1)
            with sp.If(is_bad == 0):
                with sp.Fori(0, NC - NR) as c:
                    sp.wait_ge(evicted, BANKS + (c + 1) * UN)
                    sp.dma_start(spill[bass.ds(c, 1), :, 0:NH * CH].rearrange("a p n -> (a p) n"),
                                 adj[:, bass.ds(c % NR, 1), 0:NH * CH].rearrange("p a n -> p (a n)")).then_inc(spilled, 16)
                    sp.wait_ge(spilled, c * 16 + 16)
                    hold(sp, "sp")
            with sp.Else():
                sp.wait_ge(g_set, 1)
                for row, tile in ((1, g_int[0]), (0, g_src)):
                    sp.dma_start(tile[:, 0:EC], edge_index[row, 0:EC * P].rearrange("(p t) -> p t", p=P)).then_inc(g_edges, 16)
                    sp.dma_start(tile[0:ET, EC:EC + 1], edge_index[row, EC * P:E].rearrange("(p t) -> p t", t=1)).then_inc(g_edges, 16)
                store_messages(0)
            sp.wait_ge(y_done, NC)
            sp.dma_start(fcW[:], fc_W).then_inc(fc_in, 16)
            sp.dma_start(fcb[:], fc_b[None, :].to_broadcast((P, N))).then_inc(fc_in, 16)

            def bring(i, j):
                sp.wait_ge(y_done, NC + (i - NR + 1))
                hold(sp, "sp")
                c = NC - 1 - i
                slot = (NC - 1 - j) % NR
                src = spill[bass.ds(c, 1), :, 0:NH * CH].rearrange("a p n -> (a p) n")
                sp.dma_start(adj[:, slot, 0:NH * CH], src).then_inc(loaded[j % NR], 16)

            with sp.If(is_bad == 0):
                with sp.Fori(1, NC // NR) as t:
                    for j in range(NR):
                        bring(t * NR + j, j)
                for i in range(NC // NR * NR, NC):
                    bring(i, i)
            with sp.Else():
                store_messages(1)
            for k, (c, w) in enumerate(ZC):
                sp.wait_ge(table_ready, k + 1)
                sp.dma_start(table[c * P:(c + w) * P, :].rearrange("(h l) f -> l h f", l=P), X[:, c:c + w, :]).then_inc(table_out, 16)
            sp.wait_ge(table_out, 16 * len(ZC))
            n = 0
            out_v = out.rearrange("(p b) n -> p b n", b=BB)
            for b in range(BB):
                for c, w in NCH:
                    sp.wait_ge(res_ready, n + 1)
                    sp.dma_start(out_v[:, b, c:c + w], res[:, n % 4, 0:w]).then_inc(stored[n % 4], 16)
                    n += 1
            for k in range(4):
                sp.wait_ge(stored[k], 16 * len(range(k, n, 4)))

        @block.gpsimd
        def _(pool):
            def iota(tile, pattern, base, mult):
                return nc.gpsimd.iota(tile, pattern=pattern, base=base, channel_multiplier=mult,
                                      allow_small_or_imprecise_dtypes=True)
            iota(iota_lo[:], [[1, P]], 0, 0)
            iota(chan_i[:], [[0, PLO]], 0, 1)
            iota(cnum[:], [[1, NC + 1]], 0, 0)
            iota(chan[:], [[0, 1]], 0, 1).then_inc(consts, 1)
            iota(iota_half[:], [[1, P]], 0, 0)
            iota(iota_l[:], [[1, P], [0, GV]], 0, 0)
            iota(iota_h[:], [[1, NH], [0, G]], 0, 0).then_inc(iotas, 1)
            iota(parity, [[0, (NC + 1) // 2], [TW, 2], [0, NH]], 0, 0)
            iota(codes, [[64, NC + 1], [1, NH]], 0, 0).then_inc(iotas, 1)
            iota(iota_dst[:], [[1, CH], [0, OP]], 0, 0)
            iota(iota_src, [[P, NH], [1, P], [0, R]], 1, 0).then_inc(iotas, 1)
            pool.wait_ge(clamped, 1)
            for b in range(BB):
                nc.gpsimd.indirect_dma_start(feat[:, b, 0:D], None, user_emb,
                    bass.IndirectOffsetOnAxis(ap=ucl[:, b:b + 1], axis=0)).then_inc(users_in, 16)
            pool.wait_ge(nodes_in, 32)
            pool.wait_ge(dis_ready, 1)
            nc.gpsimd.tensor_tensor(X0, X0, dis_w, ALU.mult).then_inc(rest_ready, 1)
            for k in range(2):
                pool.wait_ge(part_out, k + 1)
                nc.gpsimd.tensor_tensor(X0, X0, parts[:, :, k, :], ALU.subtract).then_inc(rest_ready, 1)
            pool.wait_ge(tab_ready, 1)
            is_bad = nc.gpsimd.value_load(bad[:], min_val=0, max_val=1)
            with pool.If(is_bad == 1):
                iota(g_hi_wide, [[1, NH], [0, D]], 0, 0).then_inc(g_wide, 1)
                for layer in range(2):
                    pool.wait_ge(g_table, 16 * (layer + 1))
                    with pool.Fori(0, TURNS_G) as i:
                        pool.wait_ge(g_staged, i + (1 + layer * TURNS_G))
                        for j in range(U):
                            pool.wait_ge(g_slot_free, i * U + (j + 1 + layer * GT))
                            pool.sem_inc(g_turn, 1)
                            nc.gpsimd.indirect_dma_start(g_rows[j], None, messages,
                                bass.IndirectOffsetOnAxis(ap=g_stage[:, j:j + 1], axis=0)).then_inc(g_rows_in[j], 16)
            pool.wait_ge(table_out, 16 * len(ZC))
            for b in range(BB):
                for c in range(CTX):
                    nc.gpsimd.indirect_dma_start(feat[:, b, D * (c + 1):D * (c + 2)], None, table,
                        bass.IndirectOffsetOnAxis(ap=ccl[:, b * CTX + c:b * CTX + c + 1], axis=0)).then_inc(rows_in[b], 16)

        @block.scalar
        def _(act):
            act.wait_ge(halves, 1)
            act.wait_ge(iotas, 1)
            made = [0]

            def low_steps(stages):
                g0, g1 = made[0], steps_by(stages)
                if g1 > g0:
                    made[0] = g1
                    with act.Fori(g0, g1) as g:
                        act.wait_ge(oh_used, g + 1)
                        for t in range(G - GV):
                            ins = nc.scalar.activation(step_lo[:, bass.ds(g % 2, 1), t, :].rearrange("p a n -> p (a n)"), iota_half[:], ACT.Sign,
                                                       bias=neg_lo[:, bass.ds(g * G + (GV + t), 1)])
                        ins.then_inc(lo_ready, 1)

            def on_turn(step, cur, stages, turns):
                low_steps(stages)
                dst = keys[1 - cur]
                _, level, left = step
                half = 1 << max(level + 1 - PLO - 1, 0)
                for q, (c, w) in enumerate(CHUNKS):
                    act.wait_ge(turned, NQ * turns + q + 1)
                    if left == "T" or level == LEVELS:
                        ins = nc.scalar.copy(dst[:, c:c + w], ps[q][:, 0:w])
                    elif half < P:
                        ins = nc.scalar.activation(dst[:, c:c + w], ps[q][:, 0:w], ACT.Copy,
                                                   scale=sign[:, level - PLO:level - PLO + 1])
                    else:
                        for b in range(w // P):
                            s = -1.0 if ((c // P + b) // (half // P)) % 2 else 1.0
                            ins = nc.scalar.mul(dst[:, c + b * P:c + (b + 1) * P], ps[q][:, b * P:(b + 1) * P], s)
                    ins.then_inc(moved, 1)
            walk(skip, on_turn)
            act.wait_ge(root_in, 1)
            nc.scalar.activation(dis[:], tmp49[:], ACT.Sqrt).then_inc(root_out, 1)

            def set_yt(layer):
                for k, (h, w) in enumerate(TH):
                    act.wait_ge(yt_turned, layer * len(TH) + k + 1)
                    nc.scalar.copy(YT[0:D3, h * P:(h + w) * P], psT[layer][k % 2][:, 0:w * P]).then_inc(yt_set, 1)
            for k in range(3):
                act.wait_ge(rest_ready, k + 1)
                nc.scalar.copy(parts[:, :, k, :], X0).then_inc(part_out, 1)
            act.wait_ge(part_out, 3)
            act.sem_inc(parts_ready, 1)
            set_yt(0)

            def chunk(c, slot, first):
                for u in range(UN):
                    w = min(2, NH - 2 * u)
                    if u == 0 and not first:
                        act.wait_ge(spilled, 16 * (c - NR + 1))
                        act.wait_ge(y_done, c - NR + 1)
                    act.wait_ge(block_done, RING + 1 + c * NH + 2 * u + w)
                    hold(act, "act")
                    nc.scalar.activation(adj8[slot][:, u * 2 * CH:(u * 2 + w) * CH],
                                         ps[u % BANKS][:, 0:w * CH], ACT.Copy, saturate=False).then_inc(evicted, 1)
            act.wait_ge(tab_ready, 1)
            is_bad = nc.scalar.value_load(bad[:], min_val=0, max_val=1)
            with act.If(is_bad == 0):
                act.sem_inc(evicted, BANKS)
                for c in range(NR):
                    chunk(c, c, True)
                with act.Fori(1, NC // NR) as t:
                    for k in range(NR):
                        chunk(t * NR + k, k, False)
                for c in range(NC // NR * NR, NC):
                    chunk(c, c % NR, False)
            with act.Else():
                for layer in range(2):
                    act.wait_ge(g_table, 16 * (layer + 1))
                    with act.Fori(0, TURNS_G) as i:
                        act.wait_ge(g_stage_free, i + (1 + layer * TURNS_G))
                        nc.scalar.copy(g_stage, g_src[:, bass.ds(i * U, U)]).then_inc(g_staged, 1)
                    if layer == 0:
                        set_yt(1)
            with act.If(is_bad == 0):
                set_yt(1)

        @block.vector
        def _(dve):
            n_chain = [0]

            def link(ins):
                n_chain[0] += 1
                ins.then_inc(chain, 1)
                dve.wait_ge(chain, n_chain[0])

            V = nc.vector
            V.memset(X0[:, FULL, :], 0.0)
            V.memset(ones16[:], 1.0)
            V.memset(ones32[:], 1.0)
            V.memset(zero_row[:], 0.0)
            V.memset(src_i[:, EC:T], 0)
            V.memset(dst_i[:, EC:T], -P).then_inc(edges_set, 1)
            dve.wait_ge(consts, 1)
            for q in range(PLO):
                V.tensor_scalar(bit_i[:, q:q + 1], chan_i[:, q:q + 1], q, 1, ALU.arith_shift_right, ALU.bitwise_and)
            V.tensor_scalar(identb[:], iota_lo[:], chan[:], None, ALU.is_equal)
            link(V.tensor_scalar(ident[:], iota_lo[:], chan[:], None, ALU.is_equal))
            link(V.tensor_scalar(sign[:], bit_i[:], -2.0, 1.0, ALU.mult, ALU.add))
            dve.wait_ge(heads_in, 32)
            for lo, cnt, src, dst, size in ((0, BB, uidx[:], ucl[:], USERS), (BB, BB * CTX, cidx[:].rearrange("p b c -> p (b c)"), ccl[:], N)):
                f, g = idx_f[:, lo:lo + cnt], neg_f[:, lo:lo + cnt]
                link(V.tensor_copy(f, src))
                link(V.tensor_scalar(g, f, 0.0, float(size), ALU.is_lt, ALU.mult))
                link(V.tensor_tensor(f, f, g, ALU.add))
                link(V.tensor_scalar(f, f, 0.0, float(size - 1), ALU.max, ALU.min))
                link(V.tensor_copy(dst, f))
            dve.sem_inc(clamped, 1)
            dve.wait_ge(edges_in, 64)
            k0, k1 = keys[0][:].bitcast(I32), keys[1][:].bitcast(I32)
            link(V.tensor_scalar(key_i[:], dst_i[:], 1, None, ALU.arith_shift_right))
            link(V.tensor_scalar(key_i[:], key_i[:], float(DEPTH), None, ALU.mult))
            link(V.tensor_scalar(k0, key_i[:], DSHIFT, None, ALU.arith_shift_right))
            link(V.scalar_tensor_tensor(out=key_i[:], in0=k0, scalar=-float(CH), in1=dst_i[:], op0=ALU.mult, op1=ALU.add))
            V.tensor_scalar(k0, k0, K_CH, None, ALU.logical_shift_left)
            V.tensor_scalar(k1, src_i[:], P - 1, GUARD, ALU.bitwise_and, ALU.bitwise_or)
            link(V.tensor_scalar(key_i[:], key_i[:], K_DST, None, ALU.logical_shift_left))
            V.tensor_tensor(k0, k0, k1, ALU.bitwise_or)
            link(V.tensor_scalar(src_i[:], src_i[:], K_BLK - PLO, 63 << K_BLK, ALU.logical_shift_left, ALU.bitwise_and))
            link(V.tensor_tensor(key_i[:], key_i[:], src_i[:], ALU.bitwise_or))
            link(V.tensor_tensor(key_i[:], key_i[:], k0, ALU.bitwise_or))
            pad = float_of_bits(GUARD | PAD_CH << K_CH | PAD_BLK << K_BLK)
            V.memset(key_i[ET:P, EC:EC + 1].bitcast(F32), pad)
            link(V.memset(key_i[:, EC + 1:T].bitcast(F32), pad))
            V.tensor_scalar(keys[0][:], key_i[:].bitcast(F32), sign[:, 0:1], None, ALU.mult).then_inc(sorted_to, 1)
            dve.wait_ge(sorted_to, 1)
            link(V.tensor_scalar(key_i[:, 0:DG * G], dst_i[:, 0:DG * G], P - 1, None, ALU.bitwise_and))
            V.tensor_copy(lo16[:], key_i[:, 0:DG * G])
            V.tensor_scalar(neg_lo[:], key_i[:, 0:DG * G], -1.0, 0.5, ALU.mult, ALU.add)
            link(V.tensor_scalar(src_i[:, 0:DG * G], dst_i[:, 0:DG * G], PLO, None, ALU.arith_shift_right))
            V.tensor_copy(hi16[:], src_i[:, 0:DG * G]).then_inc(halves, 1)
            dve.wait_ge(halves, 1)
            dve.wait_ge(iotas, 1)

            def exchange(o_low, o_high, low, high, turned_sign):
                if turned_sign:
                    V.scalar_tensor_tensor(out=o_low, in0=high, scalar=-1.0, in1=low, op0=ALU.mult, op1=ALU.min)
                    return V.scalar_tensor_tensor(out=o_high, in0=high, scalar=-1.0, in1=low, op0=ALU.mult, op1=ALU.max)
                V.tensor_tensor(o_low, low, high, ALU.min)
                return V.tensor_tensor(o_high, low, high, ALU.max)

            def on_stage(step, cur, stages, turns):
                one_hots(stages, 1)
                _, level, bit, mirror, domain = step
                s, t = keys[cur], keys[1 - cur]
                dve.wait_ge(sorted_to, stages + 1)
                dve.wait_ge(moved, NQ * turns) if turns else None
                h = 1 << (bit if domain == "T" else bit - PLO)
                whole = T // (2 * h)
                rest = T - whole * 2 * h
                neg = mirror and domain == "J"
                way = slice(None, None, -1) if mirror else slice(None)
                if whole:
                    sv = s[:, 0:whole * 2 * h].rearrange("p (q two h) -> p q two h", two=2, h=h)
                    tv = t[:, 0:whole * 2 * h].rearrange("p (q two h) -> p q two h", two=2, h=h)
                    ins = exchange(tv[:, :, 0, :], tv[:, :, 1, way], sv[:, :, 0, :], sv[:, :, 1, way], neg)
                if rest:
                    o = whole * 2 * h
                    w = max(rest - h, 0)
                    a = o + (h - w if mirror else 0)
                    if w:
                        ins = exchange(t[:, a:a + w], t[:, o + h:o + rest][:, way], s[:, a:a + w], s[:, o + h:o + rest][:, way], neg)
                    c0, c1 = (o, o + min(rest, h) - w) if mirror or not w else (o + w, o + h)
                    if c1 > c0:
                        ins = V.tensor_copy(t[:, c0:c1], s[:, c0:c1])
                ins.then_inc(sorted_to, 1)

            made = [0]

            def one_hots(stages, ahead):
                while made[0] < min(DG, steps_by(stages) + ahead):
                    g = made[0]
                    if g >= HR:
                        dve.wait_ge(oh_used, g - HR + 3)
                    V.tensor_tensor(oh_hi[:, g % HR, :, :], iota_h[:], hi16[:, g * G:(g + 1) * G].rearrange("p (o r) -> p o r", o=1).to_broadcast((P, NH, G)),
                                    ALU.is_equal)
                    V.tensor_tensor(oh_lo[:, g % HR, :, :], iota_l[:], lo16[:, g * G:g * G + GV].rearrange("p (o r) -> p o r", o=1).to_broadcast((P, P, GV)),
                                    ALU.is_equal).then_inc(hi_ready, 1)
                    made[0] += 1
            walk(on_stage, lambda step, cur, stages, turns: one_hots(stages, HR))
            dve.wait_ge(iotas, 3)
            dve.wait_ge(sorted_to, STAGES + 1)
            rows = sorted_rows[:].rearrange("p (j t) -> p j t", t=P)
            same = dst_i[:, 0:JH * (P - MULT)].bitcast(F32).rearrange("p (j t) -> p j t", t=P - MULT)
            dve.wait_ge(deg_sum, 1)
            link(V.tensor_copy(cum[:], psD[0:NH, 0:P]))
            V.tensor_tensor(count[:, 1:P], cum[:, 1:P], cum[:, 0:P - 1], ALU.subtract)
            link(V.tensor_tensor(count[:, 0:1], cum[:, 0:1], cum[:, P - 1:P], ALU.add))
            V.scalar_tensor_tensor(out=count[:], in0=psD[0:NH, P:2 * P], scalar=2.0, in1=count[:], op0=ALU.mult, op1=ALU.add).then_inc(cum_out, 1)
            link(V.tensor_tensor(same, rows[:, :, MULT:P], rows[:, :, 0:P - MULT], ALU.is_equal))
            V.scalar_tensor_tensor(out=same, in0=rows[:, :, MULT:P], scalar=pad, in1=same, op0=ALU.is_lt, op1=ALU.mult,
                                   accum_out=dup[:]).then_inc(dup_ready, 1)
            dve.wait_ge(dup_ready, 1)
            dve.wait_ge(deg_sum, 3)
            link(V.tensor_scalar(deg[:], psD[:, 256:256 + NH], 0.5, 1.0, ALU.mult, ALU.add))
            V.reciprocal(tmp49[:], deg[:]).then_inc(root_in, 1)
            dve.wait_ge(root_out, 1)
            link(V.tensor_tensor(tmp49[:], dis[:], dis[:], ALU.mult))
            link(V.tensor_tensor(tmp49[:], tmp49[:], deg[:], ALU.mult))
            link(V.tensor_scalar(tmp49[:], tmp49[:], -0.5, 1.5, ALU.mult, ALU.add))
            V.tensor_tensor(dis[:], dis[:], tmp49[:], ALU.mult).then_inc(dis_ready, 1)
            link(V.tensor_scalar(last_i[:], rows[:, :, P - 1].bitcast(I32), K_BLK, 2047, ALU.arith_shift_right, ALU.bitwise_and))
            link(V.tensor_copy(last_code[:], last_i[:]))
            for j in range(JH):
                if j >= 2:
                    dve.wait_ge(counted, j - 1)
                V.tensor_scalar(before[:, j % 2, :], codes, last_code[:, j:j + 1], None, ALU.is_gt).then_inc(before_ready, 1)
            dve.wait_ge(moved, NQ * TURNS)
            sk = sorted_keys[:].bitcast(I32)
            V.tensor_scalar(dst_i[:], sk, K_DST, 255, ALU.arith_shift_right, ALU.bitwise_and)
            V.tensor_scalar(src_i[:], sk, K_BLK - PLO, 63 << PLO, ALU.arith_shift_right, ALU.bitwise_and)
            link(V.tensor_scalar(key_i[:], sk, P - 1, None, ALU.bitwise_and))
            V.tensor_copy(dst16[:], dst_i[:])
            link(V.tensor_tensor(src_i[:], src_i[:], key_i[:], ALU.bitwise_or))
            V.tensor_scalar(src16[:], src_i[:], 1.0, None, ALU.add)
            link(V.tensor_scalar(key_i[:], sk, K_CH, 31, ALU.arith_shift_right, ALU.bitwise_and))
            link(V.tensor_copy(chunk16[:], key_i[:]))

            dve.wait_ge(counted, JH)
            for k, (c, w) in enumerate(TC):
                ins = V.tensor_copy(tau[:, c:c + w], psC[k])
            link(ins)
            tv = tau[:, 0:NB].rearrange("p (c b) -> p c b", b=NH)
            nxt = tau[:, NH:NB + NH].rearrange("p (c b) -> p c b", b=NH)[:, :, 0:1]
            par = parity[:, 0:NB].rearrange("p (c b) -> p c b", b=NH)
            link(V.tensor_tensor(par, par, tv[:, :, 0:1].to_broadcast((1, NC, NH)), ALU.subtract))
            V.tensor_tensor(tab[:, :, :, 0:GB], tv.rearrange("p c (g j) -> p c g j", j=GB),
                            par.rearrange("p c (g j) -> p c g j", j=GB), ALU.add)
            link(V.tensor_copy(tab[:, :, :, GB], nxt.to_broadcast((1, NC, NG))))
            diff = key_i[0:1, 0:NB].bitcast(F32)
            chunk_diff = key_i[0:1, NB:NB + NC].bitcast(F32)
            V.tensor_copy(worst[:, 3:4], psD[0:1, 400:401])
            link(V.tensor_tensor(diff, tau[:, 1:NB + 1], tau[:, 0:NB], ALU.subtract))
            V.tensor_reduce(worst[:, 0:1], diff, axis=mybir.AxisListType.X, op=ALU.max)
            link(V.tensor_tensor(chunk_diff, nxt, tv[:, :, 0:1], ALU.subtract))
            link(V.tensor_reduce(worst[:, 1:2], chunk_diff, axis=mybir.AxisListType.X, op=ALU.max))
            link(V.tensor_scalar(worst[:, 0:1], worst[:, 0:1], -float(R - 1), None, ALU.add))
            link(V.tensor_scalar(worst[:, 1:2], worst[:, 1:2], -float(TW - R), None, ALU.add))
            link(V.tensor_tensor(worst[:, 0:1], worst[:, 0:1], worst[:, 1:2], ALU.max))
            link(V.tensor_tensor(worst[:, 0:1], worst[:, 0:1], worst[:, 3:4], ALU.max))
            link(V.tensor_scalar(bad[:], worst[:, 0:1], 0.0, None, ALU.is_gt))
            dve.sem_inc(tab_ready, 1)
            dve.sem_inc(y_added, NR)
            regs = [dve.alloc_register(f"visit{k}") for k in range(8 * LG)]

            def general(layer):
                V.tensor_tensor(g_x, parts[:, :, 1, :], parts[:, :, 2, :], ALU.add).then_inc(g_added, 1)
                dve.wait_ge(g_added, 1 + layer * (NH + 1))
                V.tensor_tensor(g_x, g_x, parts[:, :, 0, :], ALU.add).then_inc(g_x_ready, 1)
                dve.wait_ge(g_wide, 1)
                with dve.Fori(0, TURNS_G) as i:
                    for j in range(U):
                        dve.wait_ge(g_rows_in[j], i * 16 + 16 * (1 + layer * TURNS_G))
                        dve.wait_ge(g_mm, i * U + (j + 1 + layer * GT))
                        V.tensor_scalar(g_oh[j % 2], iota_lo[:], g_lo[:, bass.ds(i * U + j, 1)], None, ALU.is_equal)
                        rows = g_rows[j].rearrange("p (o f) -> p o f", o=1).to_broadcast((P, NH, D))
                        V.scalar_tensor_tensor(out=g_spread[j % 2], in0=g_hi_wide, scalar=g_hi[:, bass.ds(i * U + j, 1)], in1=rows,
                                               op0=ALU.is_equal, op1=ALU.mult).then_inc(g_spread_ready, 1)
                        dve.wait_ge(g_spread_ready, i * U + (j + 1 + layer * GT))
                        dve.sem_inc(g_slot_free, 1)
                    dve.sem_inc(g_stage_free, 1)
                dve.wait_ge(g_summed, layer + 1)
                for k, (c, w) in enumerate(ZC):
                    ins = V.tensor_copy(g_y[:, c:c + w, :], ps[k][:, 0:w * D].rearrange("p (h f) -> p h f", f=D))
                ins.then_inc(g_y_ready, 1)
                for h in range(NH):
                    dve.wait_ge(g_turned, layer * NH + h + 1)
                    y = YT[0:D, h * P:(h + 1) * P]
                    V.tensor_tensor(y, y, psY[0:D, h % 2, 0:P], ALU.add).then_inc(g_added, 1)
                dve.wait_ge(g_added, (layer + 1) * (NH + 1))
                dve.sem_inc(y_added, NC)

            def next_window(c, base):
                return V.scalar_tensor_tensor(out=window[:, bass.ds(c % 2 * TW, TW)],
                                              in0=chunk16[:, bass.ds(base, TW)], scalar=cnum[:, bass.ds(c, 1)], in1=src16[:, bass.ds(base, TW)],
                                              op0=ALU.is_equal, op1=ALU.mult).then_inc(win_ready, 1)

            def next_hot(c, base, g):
                o = hot_v[:, :, bass.ds(c % 2 * TW + g * OP, OP)]
                return V.tensor_tensor(o, iota_dst[:], dst16[:, bass.ds(base + g * OP, OP)].rearrange("p (o t) -> p o t", o=1).to_broadcast((P, CH, OP)),
                                       ALU.is_equal).then_inc(hot_ready, 1)

            def add_y(c, count):
                dve.wait_ge(y_done, count)
                y = YT[0:D3, bass.ds(c * CH, CH)]
                V.tensor_tensor(y, y, psY[0:D3, bass.ds(c % NR, 1), 0:CH].rearrange("p a n -> p (a n)"), ALU.add).then_inc(y_added, 1)

            def chunk(c, first, last):
                for g in range(NG):
                    if g % LG == 0:
                        n = min(LG, NG - g)
                        V.load(regs[0:8 * n], tab[0:1, bass.ds(c, 1), g:g + n, :].rearrange("p a g j -> p (a g j)"))
                        visit = [dve.snap(r, min_val=0, max_val=2 * TW - R) for k, r in enumerate(regs[0:8 * n]) if k % 8 < GB]
                        if g == 0:
                            base = dve.snap(regs[GB], min_val=0, max_val=T - TW)
                    at = visit[g % LG * GB:]
                    if g and not last:
                        if g == 1:
                            dve.wait_ge(block_done, RING + 1 + c * NH)
                            next_window(c + 1, base)
                        next_hot(c + 1, base, g - 1)
                    if g == 3 and not first:
                        add_y(c - 1, c)
                    if g == 0:
                        dve.wait_ge(win_ready, c + 1)
                    for j in range(GB):
                        b = g * GB + j
                        dve.wait_ge(block_done, c * NH + (b + 1 if b < RING else b + 2))
                        V.tensor_tensor(oh_src[:, place(b), :, :], iota_src[:, b, :, :],
                                        window[:, bass.ds(at[j], R)].rearrange("p (o r) -> p o r", o=1).to_broadcast((P, P, R)),
                                        ALU.is_equal).then_inc(src_ready, 1)
            is_bad = nc.vector.value_load(bad[:], min_val=0, max_val=1)
            with dve.If(is_bad == 0):
                next_window(0, 0)
                for g in range(NPC):
                    next_hot(0, 0, g)
                dve.wait_ge(yt_set, len(TH))
                chunk(0, True, False)
                with dve.Fori(1, NC - 1) as c:
                    chunk(c, False, False)
                chunk(NC - 1, False, True)
                add_y(NC - 1, NC)
            with dve.Else():
                dve.wait_ge(yt_set, len(TH))
                V.memset(g_zero, 0.0)
                V.memset(g_src[:, EC:GT], 0)
                V.memset(g_int[0][:, EC:GT], -P).then_inc(g_set, 1)
                dve.wait_ge(g_edges, 64)
                dve.wait_ge(g_set, 1)
                for k, (shift, mask, o) in enumerate(((0, P - 1, g_lo), (PLO, -1, g_hi))):
                    if k:
                        dve.wait_ge(g_parted, 2 * k)
                    V.tensor_scalar(g_int[1], g_int[0], shift, mask, ALU.arith_shift_right, ALU.bitwise_and).then_inc(g_parted, 1)
                    dve.wait_ge(g_parted, 2 * k + 1)
                    V.tensor_copy(o, g_int[1]).then_inc(g_parted, 1)
                dve.wait_ge(g_parted, 4)
                general(0)

            def finish(layer, k):
                c, w = ZC[k]
                x = X[:, c:c + w, :]
                dve.wait_ge(z_done, layer * len(ZC) + k + 1)
                link(V.tensor_tensor(x, ps[k][:, 0:w * D].rearrange("p (h f) -> p h f", f=D), dis_w[:, c:c + w, :], ALU.mult))
                return V.tensor_tensor(x, x, bias[:, layer:layer + 1, :].to_broadcast((P, w, D)), ALU.add)
            dve.wait_ge(weights_in, 16 * 8)
            for k, (c, w) in enumerate(ZC):
                x = X[:, c:c + w, :]
                link(finish(0, k))
                link(V.scalar_tensor_tensor(out=x, in0=x, scalar=0.0, in1=dis_w[:, c:c + w, :], op0=ALU.max, op1=ALU.mult))
                for part in range(2):
                    link(V.tensor_copy(parts[:, c:c + w, part, :], x))
                    link(V.tensor_tensor(x, x, parts[:, c:c + w, part, :], ALU.subtract))
                V.tensor_copy(parts[:, c:c + w, 2, :], x).then_inc(parts_ready, 1)
            dve.wait_ge(yt_set, 2 * len(TH))
            is_bad = nc.vector.value_load(bad[:], min_val=0, max_val=1)
            with dve.If(is_bad == 0):
                with dve.Fori(0, NC) as i:
                    dve.wait_ge(y_done, NC + (i + 1))
                    hold(dve, "dve")
                    y = YT[0:D3, bass.ds((NC - 1 - i) * CH, CH)]
                    V.tensor_tensor(y, y, psY[0:D3, bass.ds((NC + i) % NR, 1), 0:CH].rearrange("p a n -> p (a n)"), ALU.add).then_inc(y_added, 1)
            with dve.Else():
                general(1)
            for k in range(len(ZC)):
                finish(1, k).then_inc(table_ready, 1)

            def copy_features(b):
                dve.wait_ge(feat_T, b + 1)
                V.tensor_copy(featT[:, b * P:(b + 1) * P], psY[:, b % 2, 0:P]).then_inc(feat_copied, 1)
            copy_features(0)
            dve.wait_ge(fc_in, 32)
            n = 0
            for b in range(BB):
                for c, w in NCH:
                    if c == NCH[TURN_AT][0] and b + 1 < BB:
                        copy_features(b + 1)
                    dve.wait_ge(fc_mm, n + 1)
                    if n >= 4:
                        dve.wait_ge(stored[n % 4], 16 * (n // 4))
                    V.tensor_tensor(res[:, n % 4, 0:w], ps[n % 4][:, 0:w], fcb[:, c:c + w], ALU.add).then_inc(res_ready, 1)
                    n += 1

        @block.tensor
        def _(pe):
            MM = nc.tensor.matmul
            pe.wait_ge(sorted_to, 1)
            pe.sem_inc(oh_used, 2)
            MM(psD[0:NH, 0:2 * P], zero_row[0:1, 0:NH], zero_row[0:1, 0:2 * P], start=True, stop=False)
            summed = [0]

            def add_steps(stages):
                g0, g1 = summed[0], steps_by(stages)
                if g1 > g0:
                    summed[0] = g1
                    with pe.Fori(g0, g1) as g:
                        pe.wait_ge(hi_ready, g + 1)
                        pe.wait_ge(lo_ready, g + 1)
                        for t in range(G):
                            low = oh_lo[:, bass.ds(g % HR, 1), :, t] if t < GV else step_lo[:, bass.ds(g % 2, 1), t - GV, :]
                            ins = MM(psD[0:NH, P:2 * P] if t < GV else psD[0:NH, 0:P], oh_hi[:, bass.ds(g % HR, 1), :, t].rearrange("p a n -> p (a n)"),
                                     low.rearrange("p a n -> p (a n)"), start=False, stop=False)
                        ins.then_inc(oh_used, 1)

            def on_turn(step, cur, stages, turns):
                src = keys[cur]
                add_steps(stages)
                pe.wait_ge(sorted_to, stages + 1)
                for q, (c, w) in enumerate(CHUNKS):
                    if turns:
                        pe.wait_ge(moved, NQ * (turns - 1) + q + 1)
                    for b in range(w // P):
                        ins = nc.tensor.transpose(ps[q][:, b * P:(b + 1) * P], src[:, c + b * P:c + (b + 1) * P], ident[:])
                    ins.then_inc(turned, 1)
            walk(skip, on_turn)
            MM(psD[0:NH, 0:2 * P], zero_row[0:1, 0:NH], zero_row[0:1, 0:2 * P], start=False, stop=True).then_inc(deg_sum, 1)
            pe.wait_ge(cum_out, 1)
            nc.tensor.transpose(psD[:, 256:256 + NH], count[:], ident[0:NH, 0:NH]).then_inc(deg_sum, 1)
            pe.wait_ge(dup_ready, 1)
            MM(psD[0:1, 400:401], ones32[:], dup[:], start=True, stop=True).then_inc(deg_sum, 1)
            pe.wait_ge(moved, NQ * TURNS)
            for j in range(JH):
                pe.wait_ge(before_ready, j + 1)
                for k, (c, w) in enumerate(TC):
                    ins = MM(psC[k], ones16[:], before[:, j % 2, c:c + w], start=(j == 0), stop=(j == JH - 1))
                ins.then_inc(counted, 1)

            def turn_parts(layer, h0, h1):
                for k, (h, w) in enumerate(TH):
                    if not h0 <= h < h1:
                        continue
                    if k >= 2:
                        pe.wait_ge(yt_set, layer * len(TH) + k - 1)
                    for b in range(w):
                        ins = nc.tensor.transpose(psT[layer][k % 2][:, b * P:(b + 1) * P], parts[:, h + b, :, :].rearrange("p k f -> p (k f)"), identb[:])
                    ins.then_inc(yt_turned, 1)
            pe.wait_ge(parts_ready, 1)
            turn_parts(0, 0, NH)
            pe.wait_ge(yt_set, len(TH))
            pe.wait_ge(tab_ready, 1)
            pe.sem_inc(block_done, RING + 1)
            regs = [pe.alloc_register(f"visit{k}") for k in range(8 * LG)]

            def general(layer):
                pe.wait_ge(g_table, 16 * (layer + 1))
                if layer == 0:
                    pe.sem_inc(g_mm, 2)
                    pe.sem_inc(g_slot_free, U)
                    pe.sem_inc(g_stage_free, 1)
                for k, (c, w) in enumerate(ZC):
                    MM(ps[k][:, 0:w * D], g_zero[:, 0:P], g_zero[:, 0:w * D], start=True, stop=False)
                with pe.Fori(0, TURNS_G) as i:
                    for j in range(U):
                        pe.wait_ge(g_spread_ready, i * U + (j + 1 + layer * GT))
                        for k, (c, w) in enumerate(ZC):
                            ins = MM(ps[k][:, 0:w * D], g_oh[j % 2], g_spread[j % 2][:, c:c + w, :].rearrange("p h f -> p (h f)"), start=False, stop=False)
                        ins.then_inc(g_mm, 1)
                for k, (c, w) in enumerate(ZC):
                    ins = MM(ps[k][:, 0:w * D], g_zero[:, 0:P], g_zero[:, 0:w * D], start=False, stop=True)
                ins.then_inc(g_summed, 1)
                pe.wait_ge(g_y_ready, layer + 1)
                for h in range(NH):
                    if h >= 2:
                        pe.wait_ge(g_added, layer * (NH + 1) + h)
                    nc.tensor.transpose(psY[0:D, h % 2, 0:P], g_y[:, h, :], ident[:]).then_inc(g_turned, 1)
                pe.wait_ge(y_added, NR + NC * (layer + 1))
                pe.sem_inc(y_done, NC)

            def aggregate(slot, order, u):
                for s in range(2 * u, min(2 * u + 2, NH)):
                    ins = MM(psY[0:D3, order % NR, 0:CH], parts[:, s, :, :].rearrange("p k f -> p (k f)"),
                             adj8[slot][:, s * CH:(s + 1) * CH], start=(s == 0), stop=(s == NH - 1))
                return ins

            def unit(c, slot, u):
                if u == 0:
                    pe.wait_ge(y_added, c + 1)
                    hold(pe, "pe")
                ins = aggregate(slot, slot, u)
                if u == UN - 1:
                    ins.then_inc(y_done, 1)

            def chunk(c, slot, first):
                for s in range(NH):
                    u = s // 2
                    if s % (LG * GB) == 0:
                        n = min(LG, (NH - s) // GB)
                        nc.tensor.load(regs[0:8 * n], tab[0:1, bass.ds(c, 1), s // GB:s // GB + n, :].rearrange("p a g j -> p (a g j)"))
                        at = [pe.snap(r, min_val=0, max_val=2 * TW - R) for k, r in enumerate(regs[0:8 * n]) if k % 8 < GB]
                    if s == 0:
                        pe.wait_ge(hot_ready, NPC * (c + 1))
                    if s % 2 == 0:
                        pe.wait_ge(evicted, c * UN + (u + 1))
                    pe.wait_ge(src_ready, c * NH + (s + 1))
                    for r in range(R):
                        ins = MM(ps[u % BANKS][:, (s % 2) * CH:(s % 2 + 1) * CH], oh_src[:, place(s), :, r],
                                 hot[:, bass.ds(at[s % (LG * GB)] + r, CH, 2 * TW)], start=(r == 0), stop=(r == R - 1))
                    ins.then_inc(block_done, 1)
                    if s % 2 == 0:
                        if u >= BANKS:
                            unit(c, slot, u - BANKS)
                        elif not first:
                            unit(c - 1, (slot - 1) % NR, UN - BANKS + u)
            is_bad = nc.tensor.value_load(bad[:], min_val=0, max_val=1)
            with pe.If(is_bad == 0):
                chunk(0, 0, True)
                with pe.Fori(0, (NC - 1) // NR) as t:
                    for k in range(1, NR + 1):
                        chunk(t * NR + k, k % NR, False)
                for u in range(UN - BANKS, UN):
                    pe.wait_ge(evicted, BANKS + (NC - 1) * UN + u + 1)
                    unit(NC - 1, (NC - 1) % NR, u)
            with pe.Else():
                general(0)

            def linear(layer, Ws, k):
                c, w = ZC[k]
                for h in range(c, c + w):
                    ins = MM(ps[k][:, (h - c) * D:(h - c + 1) * D], YT[0:D3, h * P:(h + 1) * P], Ws[:], start=True, stop=True)
                ins.then_inc(z_done, 1)
            pe.wait_ge(weights_in, 16 * 8)
            pe.wait_ge(y_added, NR + NC)
            for k in range(len(ZC) + 2):
                if k < len(ZC):
                    linear(0, W1s, k)
                if k >= 2:
                    pe.wait_ge(parts_ready, k)
                    turn_parts(1, ZC[k - 2][0], sum(ZC[k - 2]))
            pe.wait_ge(yt_set, 2 * len(TH))

            def again(i, j, first):
                pe.wait_ge(y_added, NC + i + 1)
                if not first:
                    pe.wait_ge(loaded[j % NR], 16 * (i // NR) if isinstance(i, int) else 16 * turn_no[0])
                hold(pe, "pe")
                for u in range(UN):
                    ins = aggregate((NC - 1 - j) % NR, NC + j, u)
                ins.then_inc(y_done, 1)
            is_bad = nc.tensor.value_load(bad[:], min_val=0, max_val=1)
            with pe.If(is_bad == 0):
                turn_no = [None]
                for j in range(NR):
                    again(j, j, True)
                with pe.Fori(1, NC // NR) as t:
                    turn_no[0] = t
                    for j in range(NR):
                        again(t * NR + j, j, False)
                for i in range(NC // NR * NR, NC):
                    again(i, i, False)
            with pe.Else():
                general(1)
            pe.wait_ge(y_added, NR + 2 * NC)
            for k in range(len(ZC)):
                linear(1, W2s, k)

            def turn_features(b):
                pe.wait_ge(rows_in[b], 16 * CTX)
                nc.tensor.transpose(psY[:, b % 2, 0:P], feat[:, b, :], ident[:]).then_inc(feat_T, 1)
            pe.wait_ge(users_in, 16 * BB)
            turn_features(0)
            pe.wait_ge(fc_in, 32)
            n = 0
            for b in range(BB):
                pe.wait_ge(feat_copied, b + 1)
                for c, w in NCH:
                    if c == NCH[TURN_AT][0] and b + 1 < BB:
                        turn_features(b + 1)
                    if n >= 4:
                        pe.wait_ge(res_ready, n - 3)
                    MM(ps[n % 4][:, 0:w], featT[:, b * P:(b + 1) * P], fcW[:, c:c + w], start=True, stop=True).then_inc(fc_mm, 1)
                    n += 1


_INS = ['r_user_idx', 'r_context_idx', 'L0_rec_edge_index', 'L0_rec_user_emb', 'L0_rec_service_emb',
        'L0_rec_W1', 'L0_rec_b1', 'L0_rec_W2', 'L0_rec_b2', 'L0_rec_fc_W', 'L0_rec_fc_b']


def kernel(**inputs):
    import numpy as _np
    import concourse.bacc as _bacc
    from concourse import mybir as _mybir
    from concourse.bass_utils import run_bass_kernel_spmd as _run

    nc = _bacc.Bacc("TRN2", target_bir_lowering=False, num_devices=1)
    arrays, args = {}, []
    for name in _INS:
        a = _np.ascontiguousarray(inputs[name])
        arrays[f"in_{name}_dram"] = a
        args.append(nc.dram_tensor(f"in_{name}_dram", a.shape, _mybir.dt.from_np(a.dtype), kind="ExternalInput").ap())
    args.append(nc.dram_tensor("out_dram", (BATCH, N), _mybir.dt.float32, kind="ExternalOutput").ap())
    gcn_kernel(nc, *args)
    r = _run(nc, [arrays], core_ids=[0])
    return r.results[0]["out_dram"]
```
